# Optimizing a Trainium2 kernel written in Bass

```python
import numpy as np
import jax
import jax.numpy as jnp

def _softmax(x, axis=-1):
    return jax.nn.softmax(x, axis=axis)

def _gelu(x):
    return jax.nn.gelu(x, approximate=True)

def _silu(x):
    return jax.nn.silu(x)

def _sigmoid(x):
    return jax.nn.sigmoid(x)

def _layernorm(x, axis=-1, eps=1e-05):
    m = jnp.mean(x, axis=axis, keepdims=True)
    v = jnp.var(x, axis=axis, keepdims=True)
    return (x - m) / jnp.sqrt(v + eps)

def _scatter_add(tgt, idx, src, axis=0):
    return tgt.at[idx].add(src)

def _segment_sum(src, seg, n):
    return jax.ops.segment_sum(src, seg, n)
kernel_name = 'mk_decoder_preln_d2_seqx_r4_f1cd04'

def setup_inputs(seed: int=0):
    np.random.seed(seed)
    _w = jnp.asarray

    def _rec_inputs():
        import jax
        import jax.numpy as jnp
        _rk = jax.random.key(seed)
        x = 7.22e-05 + 1 * jax.random.normal(jax.random.fold_in(_rk, 1), (32, 112, 256), jnp.float32)
        _lenS = 112 - jax.random.randint(jax.random.fold_in(_rk, 7), (32,), 0, max(1, 112 // 4) + 1, jnp.int32)
        _lenS2 = 375 - jax.random.randint(jax.random.fold_in(_rk, 8), (32,), 0, max(1, 375 // 4) + 1, jnp.int32)
        _ctx_1024P = jax.random.normal(jax.random.fold_in(_rk, 11), (32, 16, 256), jnp.float32)
        _ctx_1024c = jax.random.dirichlet(jax.random.fold_in(_rk, 511), 0.3 * jnp.ones((16,), jnp.float32), (32, 375))
        _ctx_1024t = jnp.einsum('bsk,bkd->bsd', _ctx_1024c, _ctx_1024P)
        _ctx_1024t = _ctx_1024t * jax.lax.rsqrt(jnp.mean(jnp.square(_ctx_1024t)) + 1e-12) * 0.953939
        ctx_1024 = 4.13588e-05 + 0.999923 * (_ctx_1024t + 0.3 * jax.random.normal(jax.random.fold_in(_rk, 611), (32, 375, 256), jnp.float32))
        _validS = jnp.arange(112)[None, :] < _lenS[:, None]
        _validS2 = jnp.arange(375)[None, :] < _lenS2[:, None]
        _causal = jnp.tril(jnp.ones((112, 112), dtype=bool))
        mask_BxS2_bk0 = jnp.logical_not(jnp.broadcast_to(_validS2[:, :], (32, 375)))
        return (x, ctx_1024, mask_BxS2_bk0)
    x, ctx_1024, mask_BxS2_bk0 = _rec_inputs()

    def _L0_attn_setup():
        import jax, jax.numpy as jnp
        import numpy as np
        D_MODEL = 256
        N_HEADS = 16
        N_KV = 4
        HEAD_DIM = D_MODEL // N_HEADS
        SEQ = 512
        BATCH = 2
        CAP = 50.0
        EPS = 1e-05
        THETA = 10000.0

        def _rms_norm(x, eps=EPS):
            return x * jax.lax.rsqrt(jnp.mean(jnp.square(x), axis=-1, keepdims=True) + eps)

        def _rope_cos_sin(seq_len, head_dim, theta=THETA):
            inv_freq = 1.0 / theta ** (jnp.arange(0, head_dim, 2, dtype=jnp.float32) / head_dim)
            freqs = jnp.arange(seq_len, dtype=jnp.float32)[:, None] * inv_freq[None, :]
            return (jnp.cos(freqs)[None, :, None, :], jnp.sin(freqs)[None, :, None, :])

        def _apply_rope(x, cos, sin):
            d = x.shape[-1] // 2
            x1, x2 = (x[..., :d], x[..., d:])
            return jnp.concatenate([x1 * cos - x2 * sin, x2 * cos + x1 * sin], axis=-1).astype(x.dtype)
        key = jax.random.key(seed)
        ks = jax.random.split(key, 5)
        s = 0.02
        return {'x': jax.random.normal(ks[0], (BATCH, SEQ, D_MODEL), dtype=jnp.float32), 'w_q': jax.random.normal(ks[1], (D_MODEL, N_HEADS * HEAD_DIM), dtype=jnp.float32) * s, 'w_k': jax.random.normal(ks[2], (D_MODEL, N_KV * HEAD_DIM), dtype=jnp.float32) * s, 'w_v': jax.random.normal(ks[3], (D_MODEL, N_KV * HEAD_DIM), dtype=jnp.float32) * s, 'w_o': jax.random.normal(ks[4], (N_HEADS * HEAD_DIM, D_MODEL), dtype=jnp.float32) * s}
    _L0_attn_all = _L0_attn_setup()
    _L0_attn_in = {k: v for k, v in _L0_attn_all.items() if k in ('w_q', 'w_k', 'w_v', 'w_o')}
    del _L0_attn_all

    def _L0_xattn_setup():
        import jax, jax.numpy as jnp
        import numpy as np
        NUM_HEADS = 16
        KEY_DIM = 64
        VALUE_DIM = 64
        D_MODEL = 256
        NEG_INF = -10000000000.0
        key = jax.random.key(seed)
        ks = jax.random.split(key, 8)
        B, T, S, D = (4, 512, 512, D_MODEL)
        w_scale = 1.0 / np.sqrt(D)
        inp = {'query': jax.random.normal(ks[0], (B, T, D), jnp.float32), 'key': jax.random.normal(ks[1], (B, S, D), jnp.float32), 'value': jax.random.normal(ks[2], (B, S, D), jnp.float32), 'Wq': jax.random.normal(ks[3], (D, NUM_HEADS * KEY_DIM), jnp.float32) * w_scale, 'bq': jnp.zeros((NUM_HEADS * KEY_DIM,), jnp.float32), 'Wk': jax.random.normal(ks[4], (D, NUM_HEADS * KEY_DIM), jnp.float32) * w_scale, 'bk': jnp.zeros((NUM_HEADS * KEY_DIM,), jnp.float32), 'Wv': jax.random.normal(ks[5], (D, NUM_HEADS * VALUE_DIM), jnp.float32) * w_scale, 'bv': jnp.zeros((NUM_HEADS * VALUE_DIM,), jnp.float32), 'Wo': jax.random.normal(ks[6], (NUM_HEADS * VALUE_DIM, D), jnp.float32) * w_scale, 'bo': jnp.zeros((D,), jnp.float32)}
        return inp
    _L0_xattn_all = _L0_xattn_setup()
    _L0_xattn_in = {k: v for k, v in _L0_xattn_all.items() if k in ('Wq', 'bq', 'Wk', 'bk', 'Wv', 'bv', 'Wo', 'bo')}
    del _L0_xattn_all

    def _L0_ffn_setup():
        import jax, jax.numpy as jnp
        import numpy as np
        LORA_DIM = 16
        LORA_TOKEN_INDEX = 1
        B, S, D, H = (4, 512, 256, 1024)
        key = jax.random.key(seed)
        ks = jax.random.split(key, 6)
        x = jax.random.normal(ks[0], (B, S, D), dtype=jnp.float32)
        W1 = jax.random.normal(ks[1], (H, D), dtype=jnp.float32) * 0.02
        b1 = jnp.zeros((H,), dtype=jnp.float32)
        W2 = jax.random.normal(ks[2], (D, H), dtype=jnp.float32) * 0.02
        b2 = jnp.zeros((D,), dtype=jnp.float32)
        scale = jnp.asarray(0.001, dtype=jnp.float32)
        return {'x': x, 'W1': W1, 'b1': b1, 'W2': W2, 'b2': b2, 'scale': scale}
    _L0_ffn_all = _L0_ffn_setup()
    _L0_ffn_in = {k: v for k, v in _L0_ffn_all.items() if k in ('W1', 'b1', 'W2', 'b2', 'scale')}
    del _L0_ffn_all

    def _L1_attn_setup():
        import jax, jax.numpy as jnp
        import numpy as np
        D_MODEL, N_HEADS, N_KV, HEAD_DIM, D_LAT = (256, 8, 2, 128, 32)
        N_REP = N_HEADS // N_KV
        B, T = (2, 512)
        key = jax.random.key(seed)
        ks = jax.random.split(key, 8)
        s = lambda fan_in: 1.0 / np.sqrt(fan_in)
        return {'x': jax.random.normal(ks[0], (B, T, D_MODEL), jnp.float32), 'wq': jax.random.normal(ks[1], (D_MODEL, N_HEADS * HEAD_DIM), jnp.float32) * s(D_MODEL), 'wk_down': jax.random.normal(ks[2], (D_MODEL, N_KV * D_LAT), jnp.float32) * s(D_MODEL), 'wv_down': jax.random.normal(ks[3], (D_MODEL, N_KV * D_LAT), jnp.float32) * s(D_MODEL), 'wk_up': jax.random.normal(ks[4], (D_LAT, HEAD_DIM), jnp.float32) * s(D_LAT), 'wv_up': jax.random.normal(ks[5], (D_LAT, HEAD_DIM), jnp.float32) * s(D_LAT), 'wo': jax.random.normal(ks[6], (N_HEADS * HEAD_DIM, D_MODEL), jnp.float32) * s(N_HEADS * HEAD_DIM)}
    _L1_attn_all = _L1_attn_setup()
    _L1_attn_in = {k: v for k, v in _L1_attn_all.items() if k in ('wq', 'wk_down', 'wv_down', 'wk_up', 'wv_up', 'wo')}
    del _L1_attn_all

    def _L1_xattn_setup():
        import jax, jax.numpy as jnp
        import numpy as np
        DIM = 256
        NUM_HEADS = 16
        HEAD_DIM = DIM // NUM_HEADS
        SCALE = HEAD_DIM ** (-0.5)
        EPS = 1e-05

        def _layernorm(x, w, b):
            mu = jnp.mean(x, axis=-1, keepdims=True)
            var = jnp.mean(jnp.square(x - mu), axis=-1, keepdims=True)
            return (x - mu) * jax.lax.rsqrt(var + EPS) * w + b

        def _split_heads(x):
            B, L, _ = x.shape
            return x.reshape(B, L, NUM_HEADS, HEAD_DIM).transpose(0, 2, 1, 3)
        key = jax.random.key(seed)
        ks = jax.random.split(key, 12)
        B, Lq, Lk = (4, 128, 512)
        inp = {'query': jax.random.normal(ks[0], (B, Lq, DIM), jnp.float32), 'context': jax.random.normal(ks[1], (B, Lk, DIM), jnp.float32), 'context_mask': jax.random.randint(ks[2], (B, Lk), 0, 2).astype(bool), 'qn_w': jnp.ones((DIM,), jnp.float32), 'qn_b': jnp.zeros((DIM,), jnp.float32), 'cn_w': jnp.ones((DIM,), jnp.float32), 'cn_b': jnp.zeros((DIM,), jnp.float32)}
        std = DIM ** (-0.5)
        for i, name in enumerate(['q', 'k', 'v', 'o']):
            inp[f'W{name}'] = jax.random.normal(ks[3 + i], (DIM, DIM), jnp.float32) * std
            inp[f'b{name}'] = jnp.zeros((DIM,), jnp.float32)
        return inp
    _L1_xattn_all = _L1_xattn_setup()
    _L1_xattn_in = {k: v for k, v in _L1_xattn_all.items() if k in ('qn_w', 'qn_b', 'cn_w', 'cn_b', 'Wq', 'bq', 'Wk', 'bk', 'Wv', 'bv', 'Wo', 'bo')}
    del _L1_xattn_all

    def _L1_ffn_setup():
        import jax, jax.numpy as jnp
        import numpy as np
        B, S, D = (8, 128, 256)
        H = 16
        DFF = 1024
        E = 4
        K = 2
        EPS = 1e-05

        def _layernorm(x, w, b):
            m = x.mean(-1, keepdims=True)
            v = ((x - m) ** 2).mean(-1, keepdims=True)
            return (x - m) / jnp.sqrt(v + EPS) * w + b

        def _encoder_layer(x, iw, ib, ow, ob, l1w, l1b, l2w, l2b, n1w, n1b, n2w, n2b):
            b, s, d = x.shape
            hd = d // H
            qkv = x @ iw.T + ib
            q, k, v = jnp.split(qkv, 3, axis=-1)
            rs = lambda t: t.reshape(b, s, H, hd).transpose(0, 2, 1, 3)
            q, k, v = (rs(q), rs(k), rs(v))
            scale = jnp.asarray(hd, x.dtype) ** 0.5
            scores = jnp.einsum('bhqd,bhkd->bhqk', q, k) / scale
            attn = jax.nn.softmax(scores, axis=-1)
            o = jnp.einsum('bhqk,bhkd->bhqd', attn, v).transpose(0, 2, 1, 3).reshape(b, s, d)
            o = o @ ow.T + ob
            x = _layernorm(x + o, n1w, n1b)
            ff = jax.nn.relu(x @ l1w.T + l1b) @ l2w.T + l2b
            return _layernorm(x + ff, n2w, n2b)
        key = jax.random.key(seed)
        ks = jax.random.split(key, 12)
        g = lambda k, shape: jax.random.normal(k, shape, dtype=jnp.float32) * 0.02
        return {'x': jax.random.normal(ks[0], (B, S, D), dtype=jnp.float32), 'in_proj_w': g(ks[1], (E, 3 * D, D)), 'in_proj_b': g(ks[2], (E, 3 * D)), 'out_proj_w': g(ks[3], (E, D, D)), 'out_proj_b': g(ks[4], (E, D)), 'ln1_w': jnp.ones((E, D), jnp.float32), 'ln1_b': jnp.zeros((E, D), jnp.float32), 'lin1_w': g(ks[5], (E, DFF, D)), 'lin1_b': g(ks[6], (E, DFF)), 'lin2_w': g(ks[7], (E, D, DFF)), 'lin2_b': g(ks[8], (E, D)), 'ln2_w': jnp.ones((E, D), jnp.float32), 'ln2_b': jnp.zeros((E, D), jnp.float32), 'gate_w': g(ks[9], (E, D)), 'gate_b': g(ks[10], (E,))}
    _L1_ffn_all = _L1_ffn_setup()
    _L1_ffn_in = {k: v for k, v in _L1_ffn_all.items() if k in ('in_proj_w', 'in_proj_b', 'out_proj_w', 'out_proj_b', 'ln1_w', 'ln1_b', 'lin1_w', 'lin1_b', 'lin2_w', 'lin2_b', 'ln2_w', 'ln2_b', 'gate_w', 'gate_b')}
    del _L1_ffn_all
    return {'x': x, 'ctx_1024': ctx_1024, 'mask_BxS2_bk0': mask_BxS2_bk0, 'L0_attn_w_q': _L0_attn_in['w_q'], 'L0_attn_w_k': _L0_attn_in['w_k'], 'L0_attn_w_v': _L0_attn_in['w_v'], 'L0_attn_w_o': _L0_attn_in['w_o'], 'L0_xattn_Wq': _L0_xattn_in['Wq'], 'L0_xattn_bq': _L0_xattn_in['bq'], 'L0_xattn_Wk': _L0_xattn_in['Wk'], 'L0_xattn_bk': _L0_xattn_in['bk'], 'L0_xattn_Wv': _L0_xattn_in['Wv'], 'L0_xattn_bv': _L0_xattn_in['bv'], 'L0_xattn_Wo': _L0_xattn_in['Wo'], 'L0_xattn_bo': _L0_xattn_in['bo'], 'L0_ffn_W1': _L0_ffn_in['W1'], 'L0_ffn_b1': _L0_ffn_in['b1'], 'L0_ffn_W2': _L0_ffn_in['W2'], 'L0_ffn_b2': _L0_ffn_in['b2'], 'L0_ffn_scale': _L0_ffn_in['scale'], 'L1_attn_wq': _L1_attn_in['wq'], 'L1_attn_wk_down': _L1_attn_in['wk_down'], 'L1_attn_wv_down': _L1_attn_in['wv_down'], 'L1_attn_wk_up': _L1_attn_in['wk_up'], 'L1_attn_wv_up': _L1_attn_in['wv_up'], 'L1_attn_wo': _L1_attn_in['wo'], 'L1_xattn_qn_w': _L1_xattn_in['qn_w'], 'L1_xattn_qn_b': _L1_xattn_in['qn_b'], 'L1_xattn_cn_w': _L1_xattn_in['cn_w'], 'L1_xattn_cn_b': _L1_xattn_in['cn_b'], 'L1_xattn_Wq': _L1_xattn_in['Wq'], 'L1_xattn_bq': _L1_xattn_in['bq'], 'L1_xattn_Wk': _L1_xattn_in['Wk'], 'L1_xattn_bk': _L1_xattn_in['bk'], 'L1_xattn_Wv': _L1_xattn_in['Wv'], 'L1_xattn_bv': _L1_xattn_in['bv'], 'L1_xattn_Wo': _L1_xattn_in['Wo'], 'L1_xattn_bo': _L1_xattn_in['bo'], 'L1_ffn_in_proj_w': _L1_ffn_in['in_proj_w'], 'L1_ffn_in_proj_b': _L1_ffn_in['in_proj_b'], 'L1_ffn_out_proj_w': _L1_ffn_in['out_proj_w'], 'L1_ffn_out_proj_b': _L1_ffn_in['out_proj_b'], 'L1_ffn_ln1_w': _L1_ffn_in['ln1_w'], 'L1_ffn_ln1_b': _L1_ffn_in['ln1_b'], 'L1_ffn_lin1_w': _L1_ffn_in['lin1_w'], 'L1_ffn_lin1_b': _L1_ffn_in['lin1_b'], 'L1_ffn_lin2_w': _L1_ffn_in['lin2_w'], 'L1_ffn_lin2_b': _L1_ffn_in['lin2_b'], 'L1_ffn_ln2_w': _L1_ffn_in['ln2_w'], 'L1_ffn_ln2_b': _L1_ffn_in['ln2_b'], 'L1_ffn_gate_w': _L1_ffn_in['gate_w'], 'L1_ffn_gate_b': _L1_ffn_in['gate_b']}

def reference(x, ctx_1024, mask_BxS2_bk0, L0_attn_w_q, L0_attn_w_k, L0_attn_w_v, L0_attn_w_o, L0_xattn_Wq, L0_xattn_bq, L0_xattn_Wk, L0_xattn_bk, L0_xattn_Wv, L0_xattn_bv, L0_xattn_Wo, L0_xattn_bo, L0_ffn_W1, L0_ffn_b1, L0_ffn_W2, L0_ffn_b2, L0_ffn_scale, L1_attn_wq, L1_attn_wk_down, L1_attn_wv_down, L1_attn_wk_up, L1_attn_wv_up, L1_attn_wo, L1_xattn_qn_w, L1_xattn_qn_b, L1_xattn_cn_w, L1_xattn_cn_b, L1_xattn_Wq, L1_xattn_bq, L1_xattn_Wk, L1_xattn_bk, L1_xattn_Wv, L1_xattn_bv, L1_xattn_Wo, L1_xattn_bo, L1_ffn_in_proj_w, L1_ffn_in_proj_b, L1_ffn_out_proj_w, L1_ffn_out_proj_b, L1_ffn_ln1_w, L1_ffn_ln1_b, L1_ffn_lin1_w, L1_ffn_lin1_b, L1_ffn_lin2_w, L1_ffn_lin2_b, L1_ffn_ln2_w, L1_ffn_ln2_b, L1_ffn_gate_w, L1_ffn_gate_b):
    import jax
    import jax.numpy as jnp

    def _L0_attn_ref(x, w_q, w_k, w_v, w_o):
        import jax, jax.numpy as jnp
        import numpy as np
        D_MODEL = 256
        N_HEADS = 16
        N_KV = 4
        HEAD_DIM = D_MODEL // N_HEADS
        SEQ = 512
        BATCH = 2
        CAP = 50.0
        EPS = 1e-05
        THETA = 10000.0

        def _rms_norm(x, eps=EPS):
            return x * jax.lax.rsqrt(jnp.mean(jnp.square(x), axis=-1, keepdims=True) + eps)

        def _rope_cos_sin(seq_len, head_dim, theta=THETA):
            inv_freq = 1.0 / theta ** (jnp.arange(0, head_dim, 2, dtype=jnp.float32) / head_dim)
            freqs = jnp.arange(seq_len, dtype=jnp.float32)[:, None] * inv_freq[None, :]
            return (jnp.cos(freqs)[None, :, None, :], jnp.sin(freqs)[None, :, None, :])

        def _apply_rope(x, cos, sin):
            d = x.shape[-1] // 2
            x1, x2 = (x[..., :d], x[..., d:])
            return jnp.concatenate([x1 * cos - x2 * sin, x2 * cos + x1 * sin], axis=-1).astype(x.dtype)
        B, S, _ = x.shape
        q = (x @ w_q).reshape(B, S, N_HEADS, HEAD_DIM)
        k = (x @ w_k).reshape(B, S, N_KV, HEAD_DIM)
        v = (x @ w_v).reshape(B, S, N_KV, HEAD_DIM)
        q = _rms_norm(q)
        k = _rms_norm(k)
        cos, sin = _rope_cos_sin(S, HEAD_DIM)
        q = _apply_rope(q, cos, sin)
        k = _apply_rope(k, cos, sin)
        rep = N_HEADS // N_KV
        k = jnp.repeat(k, rep, axis=2)
        v = jnp.repeat(v, rep, axis=2)
        scores = jnp.einsum('bqhd,bkhd->bhqk', q, k) / np.sqrt(HEAD_DIM).astype(np.float32)
        scores = jnp.tanh(scores.astype(jnp.float32) / CAP) * CAP
        causal = jnp.tril(jnp.ones((S, S), dtype=bool))
        scores = jnp.where(causal[None, None], scores, -jnp.inf)
        probs = jax.nn.softmax(scores, axis=-1)
        y = jnp.einsum('bhqk,bkhd->bqhd', probs, v).reshape(B, S, N_HEADS * HEAD_DIM)
        return y @ w_o

    def _L0_xattn_ref(query, key, value, Wq, bq, Wk, bk, Wv, bv, Wo, bo):
        import jax, jax.numpy as jnp
        import numpy as np
        NUM_HEADS = 16
        KEY_DIM = 64
        VALUE_DIM = 64
        D_MODEL = 256
        NEG_INF = -10000000000.0
        B, T, _ = query.shape
        S = key.shape[1]
        H, Dk, Dv = (NUM_HEADS, KEY_DIM, VALUE_DIM)
        q = (query @ Wq + bq).reshape(B, T, H, Dk)
        k = (key @ Wk + bk).reshape(B, S, H, Dk)
        v = (value @ Wv + bv).reshape(B, S, H, Dv)
        q = q * (1.0 / jnp.sqrt(jnp.asarray(Dk, q.dtype)))
        scores = jnp.einsum('bthd,bshd->bhts', q, k)
        causal = jnp.tril(jnp.ones((T, S), scores.dtype))
        scores = scores + NEG_INF * (1.0 - causal)
        attn = jax.nn.softmax(scores, axis=-1)
        ctx = jnp.einsum('bhts,bshd->bthd', attn, v).reshape(B, T, H * Dv)
        out = ctx @ Wo + bo
        return out

    def _L0_ffn_ref(x, W1, b1, W2, b2, scale):
        import jax, jax.numpy as jnp
        import numpy as np
        LORA_DIM = 16
        LORA_TOKEN_INDEX = 1
        B, S, D, H = (4, 512, 256, 1024)
        Bx, Sx, Dx = x.shape
        Hx = W1.shape[0]
        lt = jax.lax.dynamic_slice_in_dim(x, LORA_TOKEN_INDEX, LORA_DIM, axis=1)
        even = lt[:, ::2, :]
        odd = lt[:, 1::2, :]
        m1 = (even[:, :4, :, None] * odd[:, :4, None, :]).reshape(Bx, Hx, Dx)
        m2 = (even[:, 4:, :, None] * odd[:, 4:, None, :]).reshape(Bx, Dx, Hx)
        h = jnp.einsum('bsd,hd->bsh', x, W1) + scale * jnp.einsum('bsd,bhd->bsh', x, m1) + b1
        h = jax.nn.gelu(h, approximate=False)
        out = jnp.einsum('bsh,oh->bso', h, W2) + scale * jnp.einsum('bsh,boh->bso', h, m2) + b2
        return out

    def _L1_attn_ref(x, wq, wk_down, wv_down, wk_up, wv_up, wo):
        import jax, jax.numpy as jnp
        import numpy as np
        D_MODEL, N_HEADS, N_KV, HEAD_DIM, D_LAT = (256, 8, 2, 128, 32)
        N_REP = N_HEADS // N_KV
        B, T = (2, 512)
        Bq, Tq, _ = x.shape
        scale = HEAD_DIM ** (-0.5)
        q = (x @ wq).reshape(Bq, Tq, N_KV, N_REP, HEAD_DIM)
        k_lat = (x @ wk_down).reshape(Bq, Tq, N_KV, D_LAT)
        v_lat = (x @ wv_down).reshape(Bq, Tq, N_KV, D_LAT)
        k = jnp.einsum('bkhl,ld->bkhd', k_lat, wk_up)
        v = jnp.einsum('bkhl,ld->bkhd', v_lat, wv_up)
        scores = jnp.einsum('bqhrd,bkhd->bhrqk', q, k) * scale
        causal = jnp.tril(jnp.ones((Tq, Tq), dtype=bool))
        scores = jnp.where(causal, scores, jnp.finfo(scores.dtype).min)
        probs = jax.nn.softmax(scores, axis=-1)
        y = jnp.einsum('bhrqk,bkhd->bqhrd', probs, v)
        y = y.reshape(Bq, Tq, N_HEADS * HEAD_DIM)
        return y @ wo

    def _L1_xattn_ref(query, context, context_mask, qn_w, qn_b, cn_w, cn_b, Wq, bq, Wk, bk, Wv, bv, Wo, bo):
        import jax, jax.numpy as jnp
        import numpy as np
        DIM = 256
        NUM_HEADS = 16
        HEAD_DIM = DIM // NUM_HEADS
        SCALE = HEAD_DIM ** (-0.5)
        EPS = 1e-05

        def _layernorm(x, w, b):
            mu = jnp.mean(x, axis=-1, keepdims=True)
            var = jnp.mean(jnp.square(x - mu), axis=-1, keepdims=True)
            return (x - mu) * jax.lax.rsqrt(var + EPS) * w + b

        def _split_heads(x):
            B, L, _ = x.shape
            return x.reshape(B, L, NUM_HEADS, HEAD_DIM).transpose(0, 2, 1, 3)
        B, Lq, _ = query.shape
        fully_masked = jnp.all(context_mask, axis=1)
        mask = context_mask.at[:, 0].set(jnp.where(fully_masked, False, context_mask[:, 0]))
        qn = _layernorm(query, qn_w, qn_b)
        cn = _layernorm(context, cn_w, cn_b)
        q = _split_heads(qn @ Wq.T + bq)
        k = _split_heads(cn @ Wk.T + bk)
        v = _split_heads(cn @ Wv.T + bv)
        logits = jnp.einsum('bhqd,bhkd->bhqk', q * SCALE, k)
        logits = jnp.where(mask[:, None, None, :], -jnp.inf, logits)
        attn = jax.nn.softmax(logits, axis=-1)
        out = jnp.einsum('bhqk,bhkd->bhqd', attn, v)
        out = out.transpose(0, 2, 1, 3).reshape(B, Lq, DIM)
        return out @ Wo.T + bo

    def _L1_ffn_ref(x, in_proj_w, in_proj_b, out_proj_w, out_proj_b, ln1_w, ln1_b, lin1_w, lin1_b, lin2_w, lin2_b, ln2_w, ln2_b, gate_w, gate_b):
        import jax, jax.numpy as jnp
        import numpy as np
        B, S, D = (8, 128, 256)
        H = 16
        DFF = 1024
        E = 4
        K = 2
        EPS = 1e-05

        def _layernorm(x, w, b):
            m = x.mean(-1, keepdims=True)
            v = ((x - m) ** 2).mean(-1, keepdims=True)
            return (x - m) / jnp.sqrt(v + EPS) * w + b

        def _encoder_layer(x, iw, ib, ow, ob, l1w, l1b, l2w, l2b, n1w, n1b, n2w, n2b):
            b, s, d = x.shape
            hd = d // H
            qkv = x @ iw.T + ib
            q, k, v = jnp.split(qkv, 3, axis=-1)
            rs = lambda t: t.reshape(b, s, H, hd).transpose(0, 2, 1, 3)
            q, k, v = (rs(q), rs(k), rs(v))
            scale = jnp.asarray(hd, x.dtype) ** 0.5
            scores = jnp.einsum('bhqd,bhkd->bhqk', q, k) / scale
            attn = jax.nn.softmax(scores, axis=-1)
            o = jnp.einsum('bhqk,bhkd->bhqd', attn, v).transpose(0, 2, 1, 3).reshape(b, s, d)
            o = o @ ow.T + ob
            x = _layernorm(x + o, n1w, n1b)
            ff = jax.nn.relu(x @ l1w.T + l1b) @ l2w.T + l2b
            return _layernorm(x + ff, n2w, n2b)
        gate_logits = x.mean(axis=1) @ gate_w.T + gate_b
        _, top_idx = jax.lax.top_k(gate_logits, K)
        gate_weights = jax.nn.softmax(gate_logits, axis=-1)
        mask = jnp.zeros_like(gate_weights).at[jnp.arange(x.shape[0])[:, None], top_idx].set(1.0)
        expert_outs = jax.vmap(_encoder_layer, in_axes=(None, 0, 0, 0, 0, 0, 0, 0, 0, 0, 0, 0, 0))(x, in_proj_w, in_proj_b, out_proj_w, out_proj_b, lin1_w, lin1_b, lin2_w, lin2_b, ln1_w, ln1_b, ln2_w, ln2_b)
        return jnp.einsum('be,ebsd->bsd', gate_weights * mask, expert_outs)
    x = x + _L0_attn_ref(_layernorm(x, axis=-1), L0_attn_w_q, L0_attn_w_k, L0_attn_w_v, L0_attn_w_o)
    x = x + _L0_xattn_ref(_layernorm(x, axis=-1), ctx_1024, ctx_1024, L0_xattn_Wq, L0_xattn_bq, L0_xattn_Wk, L0_xattn_bk, L0_xattn_Wv, L0_xattn_bv, L0_xattn_Wo, L0_xattn_bo)
    x = x + _L0_ffn_ref(_layernorm(x, axis=-1), L0_ffn_W1, L0_ffn_b1, L0_ffn_W2, L0_ffn_b2, L0_ffn_scale)
    x = x + _L1_attn_ref(_layernorm(x, axis=-1), L1_attn_wq, L1_attn_wk_down, L1_attn_wv_down, L1_attn_wk_up, L1_attn_wv_up, L1_attn_wo)
    x = x + _L1_xattn_ref(_layernorm(x, axis=-1), ctx_1024, mask_BxS2_bk0, L1_xattn_qn_w, L1_xattn_qn_b, L1_xattn_cn_w, L1_xattn_cn_b, L1_xattn_Wq, L1_xattn_bq, L1_xattn_Wk, L1_xattn_bk, L1_xattn_Wv, L1_xattn_bv, L1_xattn_Wo, L1_xattn_bo)
    x = x + _L1_ffn_ref(_layernorm(x, axis=-1), L1_ffn_in_proj_w, L1_ffn_in_proj_b, L1_ffn_out_proj_w, L1_ffn_out_proj_b, L1_ffn_ln1_w, L1_ffn_ln1_b, L1_ffn_lin1_w, L1_ffn_lin1_b, L1_ffn_lin2_w, L1_ffn_lin2_b, L1_ffn_ln2_w, L1_ffn_ln2_b, L1_ffn_gate_w, L1_ffn_gate_b)
    return x

_drawn_inputs = setup_inputs


def setup_inputs(seed=0):
    import zlib

    import numpy as np

    out = dict(_drawn_inputs(seed))
    spreads = {'L0_xattn_bq': (0.0, 0.1),
     'L0_xattn_bk': (0.0, 2.0),
     'L0_xattn_bv': (0.0, 0.1),
     'L0_xattn_bo': (0.0, 0.1),
     'L0_ffn_b1': (0.0, 0.322),
     'L0_ffn_b2': (0.0, 0.1),
     'L1_xattn_qn_w': (1.0, 0.6),
     'L1_xattn_qn_b': (0.0, 0.759),
     'L1_xattn_cn_w': (1.0, 0.2),
     'L1_xattn_cn_b': (0.0, 0.1),
     'L1_xattn_bq': (0.0, 0.56),
     'L1_xattn_bk': (0.0, 2.0),
     'L1_xattn_bv': (0.0, 0.1),
     'L1_xattn_bo': (0.0, 0.1),
     'L1_ffn_ln1_w': (1.0, 0.2),
     'L1_ffn_ln1_b': (0.0, 0.457),
     'L1_ffn_ln2_w': (1.0, 0.2),
     'L1_ffn_ln2_b': (0.0, 0.439)}
    factors = {'L0_attn_w_q': 4.402,
     'L0_attn_w_k': 4.36,
     'L0_attn_w_v': 2.679,
     'L1_ffn_in_proj_w': 3.989,
     'L1_ffn_in_proj_b': 8.0,
     'L1_ffn_out_proj_w': 4.019,
     'L1_ffn_out_proj_b': 27.366,
     'L1_ffn_lin1_b': 39.155,
     'L1_ffn_lin2_b': 8.0,
     'L1_ffn_gate_b': 5.896}
    for name, (base, spread) in spreads.items():
        noise = np.random.default_rng([zlib.crc32(name.encode()), seed]).standard_normal(out[name].shape)
        drawn = base * np.exp(spread * noise) if base else spread * noise
        out[name] = jnp.asarray(drawn.astype(out[name].dtype))
    for name, factor in factors.items():
        out[name] = (out[name] * factor).astype(out[name].dtype)
    return out
```

```python
from contextlib import ExitStack

import concourse.bass as bass
from concourse import mybir

F32 = mybir.dt.float32
BF16 = mybir.dt.bfloat16
U32 = mybir.dt.uint32
I32 = mybir.dt.int32
ALU = mybir.AluOpType
ACT = mybir.ActivationFunctionType
AX_X = mybir.AxisListType.X

B, T, D = 32, 112, 256
LC, KT3, KP = 375, 3, 125
C2 = D // 128
H = 16
EPS = 1e-5
NEG = -1e30
CAP = 50.0
E, TOPK, DFF = 4, 2, 1024
FT = DFF // 128
QW = 4 * T

WA_PARTS = [("qkv0", C2 * 384), ("o0", C2 * D), ("xq", C2 * DFF), ("xk", C2 * DFF), ("xv", C2 * DFF), ("xo", FT * D),
            ("f1", C2 * DFF), ("f2", FT * D), ("k1", C2 * D), ("v1", C2 * 64), ("yq", C2 * D), ("yk", C2 * D),
            ("yv", C2 * D), ("yo", C2 * D), ("gate", C2 * E)]
CA_PARTS = [("xbq", FT), ("xbk", FT), ("xbv", FT), ("fb1", FT), ("qnw", C2), ("qnb", C2), ("cnw", C2), ("cnb", C2),
            ("ybq", C2), ("ybk", C2), ("ybv", C2), ("scale", 1)]
RA_PARTS = [("xbo", D), ("fb2", D), ("ybo", D)]
WE_PARTS = [("qkv", C2 * 3 * D), ("o", C2 * D), ("l1", C2 * DFF), ("l2", FT * D), ("bq", C2), ("bk", C2), ("bv", C2),
            ("b1", FT)]
RE_PARTS = [("ob", D), ("n1w", D), ("n1b", D), ("l2b", D), ("n2w", D), ("n2b", D)]
K_PARTS = [("ident", 128), ("hm8", 8 * T), ("hm8q", 8 * T), ("tri", T), ("cos", 16), ("sin", 16), ("ones", 1)]


def offsets(parts):
    at, out = 0, {}
    for name, w in parts:
        out[name] = (at, at + w)
        at += w
    return out, at


WA, NWA = offsets(WA_PARTS)
CA, NCA = offsets(CA_PARTS)
RA, NRA = offsets(RA_PARTS)
WE, NWE = offsets(WE_PARTS)
RE, NRE = offsets(RE_PARTS)
KC, NKC = offsets(K_PARTS)
NRT = 2 * B + B + E * E + 1 + E
SLOTS = (0, 1)


class Tally:

    def __init__(self, eng):
        self.eng, self.seen = eng, {}

    def wait(self, sem, n=1):
        self.seen[sem.num] = self.seen.get(sem.num, 0) + n
        self.eng.wait_ge(sem, self.seen[sem.num])

    def skip(self, sem, n):
        self.seen[sem.num] = self.seen.get(sem.num, 0) + n


def build(nc, x, ctx, mask, wa, ca, ra, up, we, re_, gb, kc, kb, rtc, out, xmid, lg, mrow, sel, stop=9, nb=B):
    with ExitStack() as es:
        def sb(name, shape, dt=F32):
            return es.enter_context(nc.sbuf_tensor(name, shape, dt))

        def sem(name):
            return es.enter_context(nc.semaphore(name))

        def pair(name):
            return [sem(f"{name}_{s}") for s in SLOTS]

        bank = [[es.enter_context(nc.psum_tensor(f"bank{s}{b}", [128, 512], F32)) for b in range(4)] for s in SLOTS]
        const = sb("const", [128, NKC])
        constb = sb("constb", [T, T + QW + T], BF16)
        ident = const[:, KC["ident"][0]:KC["ident"][1]]
        hm8 = const[:, KC["hm8"][0]:KC["hm8"][1]].rearrange("p (h q) -> p h q", h=8)
        hm8q = const[:, KC["hm8q"][0]:KC["hm8q"][1]].rearrange("p (h q) -> p h q", h=8)
        tri = const[0:T, KC["tri"][0]:KC["tri"][1]]
        cos = const[0:T, KC["cos"][0]:KC["cos"][1]]
        sin = const[0:T, KC["sin"][0]:KC["sin"][1]]
        identb, causalb, onesb = constb[:, 0:T], constb[:, T:T + QW], constb[0:1, T + QW:T + QW + T]

        loaded = sem("loaded")
        prep = sem("prep")
        prep_dma = sem("prep_dma")
        go = sem("go")
        halves_ready = sem("halves_ready")
        first = engines_done = sem("engines_done")
        x_in, c_in, m_in, x_out, lg_out = pair("x_in"), pair("c_in"), pair("m_in"), pair("x_out"), pair("lg_out")
        ln_var, ln_rstd, xn_ready, xt_psum, xt_ready = (pair("ln_var"), pair("ln_rstd"), pair("xn_ready"),
                                                        pair("xt_psum"), pair("xt_ready"))
        vec_done, act_done, pool_done = pair("vec_done"), pair("act_done"), pair("pool_done")
        proj_psum, proj_vec, proj_act = pair("proj_psum"), pair("proj_vec"), pair("proj_act")
        sq_ready, rms_var, rms_rstd, rope_ready = pair("sq_ready"), pair("rms_var"), pair("rms_rstd"), pair("rope_ready")
        qk_psum, qk_copied, masked_ready = pair("qk_psum"), pair("qk_copied"), pair("masked_ready")
        s_psum, s_shifted, p_ready, pt_psum, pt_ready = (pair("s_psum"), pair("s_shifted"), pair("p_ready"),
                                                         pair("pt_psum"), pair("pt_ready"))
        tanh_ready, o_psum, on_ready, ot_psum, ot_ready = (pair("tanh_ready"), pair("o_psum"), pair("on_ready"),
                                                           pair("ot_psum"), pair("ot_ready"))
        y_psum, x_ready = pair("y_psum"), pair("x_ready")
        pv_done, ox_psum = pair("pv_done"), pair("ox_psum")
        sel_psum, ev_ready, g_psum, g_ready, h_psum, h_ready = (pair("sel_psum"), pair("ev_ready"), pair("g_psum"),
                                                                pair("g_ready"), pair("h_psum"), pair("h_ready"))
        cn_ready, ct_psum, ct_ready = pair("cn_ready"), pair("ct_psum"), pair("ct_ready")
        mean_psum, mean_ready, logit_psum, logit_ready = (pair("mean_psum"), pair("mean_ready"), pair("logit_psum"),
                                                          pair("logit_ready"))
        last = logit_ready[1]
        step_sems = range(first.num, last.num + 1)

        with ExitStack() as phase:
            def sa(name, shape, dt=F32):
                return phase.enter_context(nc.sbuf_tensor(name, shape, dt))

            def two(name, shape, dt=F32):
                return [sa(f"{name}{s}", shape, dt) for s in SLOTS]

            w = sa("wa_sb", [128, NWA])
            col = sa("ca_sb", [128, NCA])
            row = sa("ra_sb", [T, NRA])
            wqa = sa("wqa", [128, C2, D])
            woa = sa("woa", [128, C2, D])
            bfold = sa("bfold", [128, 16])
            bq8 = sa("bq8", [128, FT])
            mwords = sa("mwords", [B, LC], I32)
            mfl = sa("mfl", [B, LC])
            mall = sa("mall", [B, 1])
            mneg = sa("mneg", [B, LC], BF16)

            X, XN, XT = two("X", [T, D]), two("XN", [T, D]), two("XT", [128, C2, T])
            CX = two("CX", [KP, KT3, D])
            CT = two("CT", [128, C2, LC])
            MR = two("MR", [1, LC], BF16)
            st6, mv, var, rstd = (two("st6", [128, 3, 6]), two("mv", [128, 3, 2]), two("var", [128, 20]),
                                  two("rstd", [128, 20]))
            SQ, QKN = two("SQ", [T, 320]), two("QKN", [T, 320])
            T2 = SQ
            QT = two("QT", [128, FT, T])
            KT = two("KT", [128, C2, LC])
            QM = two("QM", [128, C2, 8, T])
            KM = two("KM", [128, FT, 2, T])
            KM4 = two("KM4", [128, C2, 4, T])
            V0 = two("V0", [T, 4, 17])
            V64 = two("V64", [T, H, 65])
            V32 = two("V32", [T, 2, 33])
            V16 = two("V16", [KP, KT3, H, 17])
            P, PT = two("P", [128, 2, QW]), two("PT", [128, 2, QW])
            mx = two("mx", [T, H])
            rec = two("rec", [T, H])
            ON = two("ON", [T, DFF])
            R = [ON[s][:, 2 * D:4 * D] for s in SLOTS]
            OT = two("OT", [128, FT, T])
            ev = [P[s][0:4, :, :].rearrange("p u n -> p (u n)")[:, 0:2 * D] for s in SLOTS]
            EV = [QM[s][0:4, :, :, :].rearrange("p c h q -> p (c h q)")[:, 0:4 * D].rearrange("p (k n) -> p k n", k=4) for s in SLOTS]
            E2 = [ON[s][0:4, :].rearrange("p (k n) -> p k n", k=4) for s in SLOTS]
            GS, G2 = two("GS", [4, T]), two("G2", [4, 4, T])
            xbar, lrow = two("xbar", [128, C2]), two("lrow", [1, E])
            upw = QM[0][:, :, :, :].rearrange("p c h q -> p (c h q)")
            upc = sa("upc", [128, 64])
            kbw = QM[1][0:T, :, :, :].rearrange("p c h q -> p (c h q)")[:, 0:T + QW + T]

            def W(name, c):
                a, b = WA[name]
                return w[:, a:b].rearrange("p (c n) -> p c n", c=c)

            def cc(name):
                a, b = CA[name]
                return col[:, a:b]

            def rr(name):
                a, b = RA[name]
                return row[:, a:b]

            qkv0, o0, xq, xk, xv, xo = W("qkv0", C2), W("o0", C2), W("xq", C2), W("xk", C2), W("xv", C2), W("xo", FT)
            f1, f2, k1, v1, gate = W("f1", C2), W("f2", FT), W("k1", C2), W("v1", C2), W("gate", C2)
            yq, yk, yv, yo = W("yq", C2), W("yk", C2), W("yv", C2), W("yo", C2)

            block = phase.enter_context(nc.Block())

            @block.sync
            def _(sp):
                t = Tally(sp)
                for dst, src in ((const[:, :], kc), (kbw, kb), (w[:, :], wa), (col[:, :], ca),
                                 (row[:, :], ra.to_broadcast((T, NRA))), (mwords[:, :], mask), (upc[:, :], up[:, 0:64])):
                    sp.dma_start(dst, src).then_inc(loaded, 16)
                for part in range(4):
                    if part:
                        t.wait(prep, 1)
                    a = 64 + part * 1024
                    sp.dma_start(upw[:, 0:1024], up[:, a:a + 1024]).then_inc(prep_dma, 16)
                sp.wait_ge(loaded, 7 * 16)
                t.wait(m_in[0], 1)
                sp.dma_start(mrow, mneg[:, :]).then_inc(loaded, 16)
                sp.wait_ge(loaded, 8 * 16)
                t.wait(m_in[1], 1)
                sp.sem_clear(step_sems).then_inc(go, 1)
                with sp.Fori(0, nb // 2) as i:
                    t = Tally(sp)
                    for s in SLOTS:
                        b = i * 2 + s
                        sp.dma_start(X[s][:, :], x[bass.ds(b, 1), :, :].rearrange("a t d -> (a t) d")).then_inc(x_in[s], 16)
                        sp.dma_start(CX[s][:, :, :], ctx[bass.ds(b, 1), :, :].rearrange("a (t p) d -> p (a t) d", p=KP)).then_inc(c_in[s], 16)
                        sp.dma_start(MR[s][:, :], mrow[bass.ds(b, 1), :]).then_inc(m_in[s], 16)
                    for s in SLOTS:
                        b = i * 2 + s
                        t.wait(logit_ready[s], 1)
                        sp.dma_start(out[bass.ds(b, 1), :, :].rearrange("a t d -> (a t) d"), X[s][:, :]).then_inc(x_out[s], 16)
                        sp.dma_start(xmid[bass.ds(b, 1), :, :].rearrange("a t d -> (a t) d"), XN[s][:, :]).then_inc(x_out[s], 16)
                        sp.dma_start(lg[bass.ds(b, 1), :], lrow[s][:, :]).then_inc(lg_out[s], 16)
                    for s in SLOTS:
                        t.wait(x_out[s], 32)
                        t.wait(lg_out[s], 16)
                    t.wait(engines_done, 4)
                    sp.sem_clear(step_sems).then_inc(go, 1)

            @block.tensor
            def _(pe):
                mm = nc.tensor.matmul
                t = Tally(pe)
                pe.wait_ge(loaded, 7 * 16)
                for part in range(4):
                    t.wait(prep_dma, 16)
                    for k in range(2):
                        h = 2 * part + k
                        for c in range(C2):
                            mm(bank[0][0][:, (c * 8 + h) * 32:(c * 8 + h) * 32 + 32], upw[:, k * D + c * 128:k * D + c * 128 + 128],
                               upc[:, 0:32], start=True, stop=True)
                        last_mm = mm(bank[0][1 + h // 4][32 * (h % 4):32 * (h % 4) + 32, 0:D], upc[:, 32:64],
                                     upw[:, 512 + k * D:512 + k * D + D], start=True, stop=True)
                    last_mm.then_inc(prep, 1)
                for n, (wt, bcol) in enumerate(((yq, "qnb"), (yk, "cnb"), (yv, "cnb"))):
                    for m in range(C2):
                        for c in range(C2):
                            last_mm = mm(bank[0][3][:, 2 * n + m:2 * n + m + 1], wt[:, c, m * 128:m * 128 + 128],
                                         cc(bcol)[:, c:c + 1], start=(c == 0), stop=(c == C2 - 1))
                last_mm.then_inc(prep, 1)
                pe.wait_ge(go, 1)
                with pe.Fori(0, nb // 2) as i:
                    t = Tally(pe)

                    def norm_transposes(s):
                        t.wait(xn_ready[s])
                        for c in range(C2):
                            m = nc.tensor.transpose(bank[s][2][:, c * T:(c + 1) * T], XN[s][:, c * 128:(c + 1) * 128], ident[0:T, 0:T])
                        m.then_inc(xt_psum[s], 1)

                    def feature_major(s, bk, wt, rhs, tiles, n):
                        for j, m in enumerate(tiles):
                            for c in range(C2):
                                r = mm(bank[s][bk][:, j * n:(j + 1) * n], wt[:, c, m * 128:(m + 1) * 128], rhs[:, c, :],
                                       start=(c == 0), stop=(c == C2 - 1))
                        r.then_inc(proj_psum[s], 1)

                    def token_major(s, bk, rows, lhs, wt, n0, n1, sig):
                        for c in range(C2):
                            r = mm(bank[s][bk][0:rows, 0:n1 - n0], lhs[:, c, :], wt[:, c, n0:n1], start=(c == 0), stop=(c == C2 - 1))
                        r.then_inc(sig[s], 1)

                    def output_projection(s, nt, wt):
                        t.wait(ot_ready[s])
                        for c in range(nt):
                            m = mm(bank[s][0][0:T, 0:D], OT[s][:, c, :], wt[:, c, :], start=(c == 0), stop=(c == nt - 1))
                        m.then_inc(y_psum[s], 1)

                    def transpose_o(s):
                        t.wait(on_ready[s])
                        for c in range(C2):
                            m = nc.tensor.transpose(bank[s][2][:, c * T:(c + 1) * T], ON[s][:, c * 128:(c + 1) * 128], ident[0:T, 0:T])
                        m.then_inc(ot_psum[s], 1)

                    for s in SLOTS:
                        norm_transposes(s)
                    for s in SLOTS:
                        t.wait(xt_ready[s])
                        token_major(s, 0, T, XT[s], qkv0, 0, 384, proj_psum)
                    for s in SLOTS:
                        t.wait(rope_ready[s])
                        for c in range(4):
                            m = nc.tensor.transpose(bank[s][2][:, c * T:(c + 1) * T], R[s][:, c * 128:(c + 1) * 128], ident[0:T, 0:T])
                        m.then_inc(qk_psum[s], 1)
                    for u in range(5):
                        for s in SLOTS:
                            if u < 4:
                                t.wait(masked_ready[s]) if u % 2 == 0 else None
                                mm(bank[s][u % 2][0:T, 0:QW], KT[s][:, u // 2, 0:T], QM[s][:, u // 2, 4 * (u % 2):4 * (u % 2) + 4, :],
                                   start=True, stop=True).then_inc(s_psum[s], 1)
                        for s in SLOTS:
                            if u > 0:
                                v = u - 1
                                t.wait(p_ready[s])
                                for h in range(4):
                                    m = mm(bank[s][3][0:T, 17 * (4 * v + h):17 * (4 * v + h) + 17], P[s][0:T, v % 2, h * T:(h + 1) * T],
                                           V0[s][:, v, :], start=True, stop=True)
                                m.then_inc(pv_done[s] if v < 3 else o_psum[s], 1)
                    for s in SLOTS:
                        transpose_o(s)
                    for s in SLOTS:
                        output_projection(s, C2, o0)
                    if stop == 1:
                        pass

                    if stop > 1:
                        for s in SLOTS:
                            t.wait(c_in[s], 16)
                            for c in range(C2):
                                m = nc.tensor.transpose(bank[s][1][:, c * T:(c + 1) * T], CX[s][0:T, 0, c * 128:(c + 1) * 128], ident[0:T, 0:T])
                            m.then_inc(ct_psum[s], 1)
                        for s in SLOTS:
                            norm_transposes(s)
                        for s in SLOTS:
                            t.wait(ct_ready[s])
                            t.wait(xt_ready[s])
                            rhs = CT[s][:, :, 0:T]
                            feature_major(s, 0, xk, rhs, range(0, 4), T)
                            feature_major(s, 1, xk, rhs, range(4, 8), T)
                        for s in SLOTS:
                            feature_major(s, 2, xq, XT[s], range(0, 4), T)
                            t.wait(proj_vec[s], 1)
                            feature_major(s, 0, xq, XT[s], range(4, 8), T)
                        for s in SLOTS:
                            t.wait(proj_vec[s], 1)
                            token_major(s, 1, T, CT[s][:, :, 0:T], xv, 0, 512, proj_psum)
                            t.wait(proj_vec[s], 1)
                            token_major(s, 2, T, CT[s][:, :, 0:T], xv, 512, 1024, proj_psum)
                        for s in SLOTS:
                            t.wait(proj_vec[s], 1)
                            t.wait(proj_act[s], 2)
                        for u in range(6):
                            for s in SLOTS:
                                if u < 4:
                                    bk = bank[s][u % 2]
                                    if u >= 2:
                                        t.wait(s_shifted[s])
                                    mm(bk[0:T, 0:QW], identb, causalb, start=True, stop=True)
                                    for k in range(2):
                                        m = mm(bk[0:T, k * 2 * T:(k + 1) * 2 * T], QT[s][:, 2 * u + k, :], KM[s][:, 2 * u + k, :, :],
                                               start=False, stop=True, skip_group_check=True)
                                    m.then_inc(s_psum[s], 1)
                            for s in SLOTS:
                                if u >= 2:
                                    v = u - 2
                                    t.wait(pt_ready[s])
                                    if v > 0:
                                        t.wait(on_ready[s])
                                    for h in range(4):
                                        m = mm(bank[s][3][0:T, 65 * h:65 * h + 65], PT[s][0:T, v % 2, h * T:(h + 1) * T],
                                               V64[s][:, 4 * v + h, :], start=True, stop=True)
                                    m.then_inc(o_psum[s], 1)
                            for s in SLOTS:
                                if 1 <= u < 5:
                                    t.wait(p_ready[s])
                                    for h in range(4):
                                        m = nc.tensor.transpose(bank[s][2][0:T, h * T:(h + 1) * T], P[s][0:T, (u - 1) % 2, h * T:(h + 1) * T], ident[0:T, 0:T])
                                    m.then_inc(pt_psum[s], 1)
                        for s in SLOTS:
                            t.wait(s_shifted[s], 2)
                            t.wait(on_ready[s])
                        for g in range(2):
                            for s in SLOTS:
                                for c in range(4):
                                    m = nc.tensor.transpose(bank[s][2 + g][:, c * T:(c + 1) * T], ON[s][:, (4 * g + c) * 128:(4 * g + c + 1) * 128], ident[0:T, 0:T])
                                m.then_inc(ox_psum[s], 1)
                        for s in SLOTS:
                            t.wait(ot_ready[s])
                            output_projection(s, FT, xo)

                    if stop > 2:
                        for s in SLOTS:
                            norm_transposes(s)
                            for k in range(2):
                                m = mm(bank[s][3][0:4, k * D:(k + 1) * D], ident[0:T, 8 * k + 1:8 * k + 9:2], XN[s][:, :],
                                       start=True, stop=True)
                            m.then_inc(sel_psum[s], 1)
                        for s in SLOTS:
                            t.wait(xt_ready[s])
                            for c in range(C2):
                                m = mm(bank[s][2][0:4, 0:T], XT[s][:, c, 2:10:2], XT[s][:, c, :], start=(c == 0), stop=(c == 1))
                            m.then_inc(g_psum[s], 1)
                        for s in SLOTS:
                            t.wait(ev_ready[s], 2)
                            t.wait(g_ready[s])
                            for g in range(2):
                                for j in range(4):
                                    o = bank[s][g][:, j * T:(j + 1) * T]
                                    mt = 4 * g + j
                                    for c in range(C2):
                                        mm(o, f1[:, c, mt * 128:(mt + 1) * 128], XT[s][:, c, :], start=(c == 0), stop=False)
                                    m = mm(o, EV[s][:, mt // 2, (mt % 2) * 128:(mt % 2) * 128 + 128], GS[s][:, :], start=False, stop=True)
                                m.then_inc(h_psum[s], 1)
                        for s in SLOTS:
                            t.wait(h_ready[s])
                            for j in range(4):
                                for c in range(C2):
                                    m = mm(bank[s][2][0:4, j * T:(j + 1) * T], XT[s][:, c, 10:18:2], QT[s][:, 2 * j + c, :], start=(c == 0), stop=(c == 1))
                            m.then_inc(g_psum[s], 1)
                            for c in range(FT):
                                mm(bank[s][3][0:T, 0:D], QT[s][:, c, :], f2[:, c, :], start=(c == 0), stop=False)
                            t.wait(g_ready[s])
                            for j in range(4):
                                m = mm(bank[s][3][0:T, 0:D], G2[s][:, j, :], E2[s][:, j, :], start=False, stop=(j == 3))
                            m.then_inc(y_psum[s], 1)

                    if stop > 3:
                        for s in SLOTS:
                            norm_transposes(s)
                        for s in SLOTS:
                            t.wait(xt_ready[s])
                            feature_major(s, 0, k1, XT[s], range(C2), T)
                            feature_major(s, 1, wqa, XT[s], range(C2), T)
                            token_major(s, 2, T, XT[s], v1, 0, 64, proj_psum)
                        for s in SLOTS:
                            t.wait(proj_vec[s])
                            t.wait(proj_act[s], 2)
                        for u in range(4):
                            for s in SLOTS:
                                if u < 2:
                                    mm(bank[s][u][0:T, 0:QW], identb, causalb, start=True, stop=False)
                                    mm(bank[s][u][0:T, 0:QW], QT[s][:, u, :], KM4[s][:, u, :, :], start=False, stop=True).then_inc(s_psum[s], 1)
                            for s in SLOTS:
                                if u >= 2:
                                    v = u - 2
                                    t.wait(pt_ready[s])
                                    for h in range(4):
                                        m = mm(bank[s][3][0:T, 33 * (4 * v + h):33 * (4 * v + h) + 33], PT[s][0:T, v, h * T:(h + 1) * T],
                                               V32[s][:, v, :], start=True, stop=True)
                                    m.then_inc(pv_done[s] if v < 1 else o_psum[s], 1)
                            for s in SLOTS:
                                if 1 <= u < 3:
                                    t.wait(p_ready[s])
                                    for h in range(4):
                                        m = nc.tensor.transpose(bank[s][2][0:T, h * T:(h + 1) * T], P[s][0:T, u - 1, h * T:(h + 1) * T], ident[0:T, 0:T])
                                    m.then_inc(pt_psum[s], 1)
                        for s in SLOTS:
                            transpose_o(s)
                        for s in SLOTS:
                            output_projection(s, C2, woa)

                    if stop > 4:
                        for s in SLOTS:
                            for k in range(KT3):
                                t.wait(cn_ready[s])
                                if k == 2:
                                    t.wait(ct_ready[s])
                                for c in range(C2):
                                    m = nc.tensor.transpose(bank[s][1 + k % 2][:, c * KP:(c + 1) * KP], CX[s][:, k, c * 128:(c + 1) * 128], ident[0:KP, 0:KP])
                                m.then_inc(ct_psum[s], 1)
                        for s in SLOTS:
                            t.wait(ct_ready[s], 2)
                            norm_transposes(s)
                        for s in SLOTS:
                            for m2 in range(C2):
                                for c in range(C2):
                                    m = mm(bank[s][m2][:, 0:LC], yk[:, c, m2 * 128:(m2 + 1) * 128], CT[s][:, c, :], start=(c == 0), stop=(c == 1))
                                m.then_inc(proj_psum[s], 1)
                        for s in SLOTS:
                            t.wait(xt_ready[s])
                            feature_major(s, 3, yq, XT[s], range(C2), T)
                            for k in range(KT3):
                                t.wait(proj_act[s])
                                bk = (0, 1, 0)[k]
                                for c in range(C2):
                                    m = mm(bank[s][bk][0:KP, 0:D], CT[s][:, c, k * KP:(k + 1) * KP], yv[:, c, :], start=(c == 0), stop=(c == 1))
                                m.then_inc(proj_psum[s], 1)
                        for s in SLOTS:
                            t.wait(proj_act[s], 2)
                            t.wait(m_in[s], 16)
                        for h in range(H + 2):
                            for s in SLOTS:
                                if h < H:
                                    bk = bank[s][h % 2]
                                    if h % 8 == 0:
                                        t.wait(masked_ready[s])
                                    mm(bk[0:T, 0:LC], onesb, MR[s][:, :], start=True, stop=False)
                                    mm(bk[0:T, 0:LC], QM[s][:, h // 8, h % 8, :], KT[s][:, h // 8, :], start=False, stop=True).then_inc(s_psum[s], 1)
                            for s in SLOTS:
                                if h >= 2:
                                    v = h - 2
                                    t.wait(pt_ready[s])
                                    for k in range(KT3):
                                        m = mm(bank[s][3][0:T, 17 * v:17 * v + 17], PT[s][0:KP, v % 2, k * T:(k + 1) * T],
                                               V16[s][:, k, v, :], start=(k == 0), stop=(k == KT3 - 1))
                                    m.then_inc(pv_done[s] if v < H - 1 else o_psum[s], 1)
                            for s in SLOTS:
                                if 1 <= h < H + 1:
                                    v = h - 1
                                    t.wait(p_ready[s])
                                    for k in range(KT3):
                                        m = nc.tensor.transpose(bank[s][2][0:KP, k * T:(k + 1) * T], P[s][0:T, v % 2, k * KP:(k + 1) * KP], ident[0:T, 0:T])
                                    m.then_inc(pt_psum[s], 1)
                        for s in SLOTS:
                            transpose_o(s)
                        for s in SLOTS:
                            output_projection(s, C2, yo)

                    for s in SLOTS:
                        t.wait(xn_ready[s])
                        for c in range(C2):
                            m = mm(bank[s][2][:, c:c + 1], XN[s][:, c * 128:(c + 1) * 128], const[0:T, KC["ones"][0]:KC["ones"][1]], start=True, stop=True)
                        m.then_inc(mean_psum[s], 1)
                    for s in SLOTS:
                        t.wait(mean_ready[s])
                        for c in range(C2):
                            m = mm(bank[s][3][0:1, 0:E], xbar[s][:, c:c + 1], gate[:, c, :], start=(c == 0), stop=(c == 1))
                        m.then_inc(logit_psum[s], 1)
                    pe.drain().then_inc(engines_done, 1)
                    pe.wait_ge(go, i + 2)

            @block.scalar
            def _(act):
                A = nc.scalar.activation
                act.wait_ge(go, 1)
                with act.Fori(0, nb // 2) as i:
                    t = Tally(act)

                    def copy_xt(s):
                        t.wait(xt_psum[s])
                        A(XT[s][:, :, :], bank[s][2][:, 0:C2 * T].rearrange("p (c q) -> p c q", c=C2), ACT.Copy).then_inc(xt_ready[s], 1)

                    def exp_units(units):
                        for u in range(units + 1):
                            for s in SLOTS:
                                if u < units:
                                    t.wait(s_shifted[s])
                                    A(P[s][0:T, u % 2, :], P[s][0:T, u % 2, :], ACT.Exp).then_inc(p_ready[s], 1)
                            for s in SLOTS:
                                if u > 0:
                                    v = u - 1
                                    t.wait(pt_psum[s])
                                    if v >= 2:
                                        t.wait(o_psum[s])
                                    A(PT[s][0:T, v % 2, :], bank[s][2][0:T, 0:QW], ACT.Copy).then_inc(pt_ready[s], 1)

                    def copy_ot(s, bias=None):
                        t.wait(ot_psum[s])
                        if bias is None:
                            A(OT[s][:, 0:C2, :], bank[s][2][:, 0:C2 * T].rearrange("p (c q) -> p c q", c=C2), ACT.Copy).then_inc(ot_ready[s], 1)
                        else:
                            A(OT[s][:, 0, :], bank[s][2][:, 0:T], ACT.Identity, bias=bias[:, 0:1])
                            A(OT[s][:, 1, :], bank[s][2][:, T:2 * T], ACT.Identity, bias=bias[:, 1:2]).then_inc(ot_ready[s], 1)

                    for s in SLOTS:
                        copy_xt(s)
                    for s in SLOTS:
                        t.wait(proj_psum[s])
                        A(SQ[s][:, :], bank[s][0][0:T, 0:320], ACT.Square)
                        A(V0[s][:, :, 0:16], bank[s][0][0:T, 320:384].rearrange("p (g d) -> p g d", g=4), ACT.Copy).then_inc(sq_ready[s], 1)
                    for s in SLOTS:
                        t.wait(qk_psum[s])
                        A(QT[s][:, 0:C2, :], bank[s][2][:, 0:C2 * T].rearrange("p (c q) -> p c q", c=C2), ACT.Copy).then_inc(qk_copied[s], 1)
                        A(KT[s][:, :, 0:T], bank[s][2][:, C2 * T:2 * C2 * T].rearrange("p (c q) -> p c q", c=C2), ACT.Copy).then_inc(qk_copied[s], 1)
                    for u in range(4):
                        for s in SLOTS:
                            t.wait(s_psum[s])
                            if u >= 2:
                                t.wait(pv_done[s])
                            A(P[s][0:T, u % 2, :], bank[s][u % 2][0:T, 0:QW], ACT.Tanh, scale=1.0 / (4.0 * CAP)).then_inc(tanh_ready[s], 1)
                        for s in SLOTS:
                            t.wait(tanh_ready[s])
                            A(P[s][0:T, u % 2, :], P[s][0:T, u % 2, :], ACT.Exp, scale=CAP).then_inc(act_done[s], 1)
                    for s in SLOTS:
                        t.skip(pv_done[s], 1)
                        t.skip(o_psum[s], 1)
                        copy_ot(s)

                    if stop > 1:
                        for s in SLOTS:
                            t.wait(ct_psum[s])
                            A(CT[s][:, :, 0:T], bank[s][1][:, 0:C2 * T].rearrange("p (c q) -> p c q", c=C2), ACT.Copy).then_inc(ct_ready[s], 1)
                        for s in SLOTS:
                            copy_xt(s)
                        for s in SLOTS:
                            for k in range(2):
                                t.wait(proj_psum[s], 5 if k == 0 else 1)
                                A(V64[s][:, 8 * k:8 * k + 8, 0:64], bank[s][1 + k][0:T, 0:512].rearrange("p (h d) -> p h d", h=8), ACT.Copy).then_inc(proj_act[s], 1)
                        exp_units(4)
                        for s in SLOTS:
                            t.skip(o_psum[s], 2)

                    if stop > 2:
                        for s in SLOTS:
                            copy_xt(s)
                            t.wait(sel_psum[s])
                            A(ev[s], bank[s][3][0:4, 0:2 * D], ACT.Copy).then_inc(ev_ready[s], 1)
                        for s in SLOTS:
                            t.wait(g_psum[s])
                            A(GS[s][:, :], bank[s][2][0:4, 0:T], ACT.Copy, scale=cc("scale")[0:4, :]).then_inc(g_ready[s], 1)
                        for s in SLOTS:
                            for g in range(2):
                                t.wait(h_psum[s])
                                for j in range(4):
                                    mt = 4 * g + j
                                    m = A(QT[s][:, mt, :], bank[s][g][:, j * T:(j + 1) * T], ACT.Gelu, bias=cc("fb1")[:, mt:mt + 1])
                            m.then_inc(h_ready[s], 1)
                        for s in SLOTS:
                            t.wait(g_psum[s])
                            A(G2[s][:, :, :], bank[s][2][0:4, 0:QW].rearrange("p (j q) -> p j q", j=4), ACT.Copy, scale=cc("scale")[0:4, :]).then_inc(g_ready[s], 1)

                    if stop > 3:
                        for s in SLOTS:
                            copy_xt(s)
                        for s in SLOTS:
                            t.wait(proj_psum[s], 2)
                            A(QT[s][:, 0:C2, :], bank[s][1][:, 0:C2 * T].rearrange("p (c q) -> p c q", c=C2), ACT.Copy, scale=128 ** -0.5).then_inc(proj_act[s], 1)
                            t.wait(proj_psum[s])
                            A(V32[s][:, :, 0:32], bank[s][2][0:T, 0:64].rearrange("p (g d) -> p g d", g=2), ACT.Copy).then_inc(proj_act[s], 1)
                        exp_units(2)
                        for s in SLOTS:
                            t.skip(pv_done[s], 1)
                            copy_ot(s)

                    if stop > 4:
                        for s in SLOTS:
                            for k in range(KT3):
                                t.wait(ct_psum[s])
                                A(CT[s][:, :, k * KP:(k + 1) * KP], bank[s][1 + k % 2][:, 0:C2 * KP].rearrange("p (c q) -> p c q", c=C2), ACT.Copy).then_inc(ct_ready[s], 1)
                        for s in SLOTS:
                            copy_xt(s)
                        for s in SLOTS:
                            for m2 in range(C2):
                                t.wait(proj_psum[s])
                                A(KT[s][:, m2, :], bank[s][m2][:, 0:LC], ACT.Identity, bias=bfold[:, 2 + m2:3 + m2]).then_inc(proj_act[s], 1)
                        for s in SLOTS:
                            t.wait(proj_psum[s])
                            for m2 in range(C2):
                                m = A(QT[s][:, m2, :], bank[s][3][:, m2 * T:(m2 + 1) * T], ACT.Identity, bias=bfold[:, 8 + m2:9 + m2], scale=0.25)
                            m.then_inc(qk_copied[s], 1)
                            for k in range(KT3):
                                t.wait(proj_psum[s])
                                m = A(V16[s][:, k, :, 0:16], bank[s][(0, 1, 0)[k]][0:KP, 0:D].rearrange("p (h d) -> p h d", h=H), ACT.Copy)
                                m.then_inc(proj_act[s], 1)
                        for h in range(H + 1):
                            for s in SLOTS:
                                if h < H:
                                    t.wait(s_shifted[s])
                                    A(P[s][0:T, h % 2, 0:LC], bank[s][h % 2][0:T, 0:LC], ACT.Exp, bias=mx[s][:, h:h + 1]).then_inc(p_ready[s], 1)
                            for s in SLOTS:
                                if h > 0:
                                    v = h - 1
                                    t.wait(pt_psum[s])
                                    if v >= 2:
                                        t.wait(pv_done[s])
                                    A(PT[s][0:KP, v % 2, 0:KT3 * T], bank[s][2][0:KP, 0:KT3 * T], ACT.Copy).then_inc(pt_ready[s], 1)
                        for s in SLOTS:
                            copy_ot(s, bfold[:, 4:6])

                    for s in SLOTS:
                        t.wait(mean_psum[s])
                        A(xbar[s][:, :], bank[s][2][:, 0:C2], ACT.Copy, scale=1.0 / T).then_inc(mean_ready[s], 1)
                    for s in SLOTS:
                        t.wait(logit_psum[s])
                        A(lrow[s][:, :], bank[s][3][0:1, 0:E], ACT.Copy).then_inc(logit_ready[s], 1)
                    act.drain().then_inc(engines_done, 1)
                    act.wait_ge(go, i + 2)

            @block.vector
            def _(dve):
                v = nc.vector
                t = Tally(dve)
                chain = vec_done[0]
                dve.wait_ge(loaded, 7 * 16)
                v.tensor_copy(constb[:, :], kbw)
                v.tensor_copy(mfl[:, :], mwords[:, :]).then_inc(chain, 1)
                t.wait(chain)
                v.tensor_reduce(mall[:, :], mfl[:, :], AX_X, ALU.min).then_inc(chain, 1)
                t.wait(chain)
                v.tensor_tensor(mfl[:, 0:1], mfl[:, 0:1], mall[:, :], ALU.subtract).then_inc(chain, 1)
                t.wait(chain)
                v.tensor_scalar(mneg[:, :], mfl[:, :], NEG, None, ALU.mult).then_inc(m_in[0], 1)
                v.tensor_scalar(bq8[:, :], cc("xbq"), 0.125, None, ALU.mult)
                dve.wait_ge(prep, 5)
                for c in range(C2):
                    v.tensor_copy(wqa[:, c, :], bank[0][0][:, c * D:(c + 1) * D])
                    v.tensor_copy(woa[:, c, :], bank[0][1 + c][:, 0:D])
                a = CA["ybq"][0]
                v.tensor_tensor(bfold[:, 0:6], bank[0][3][:, 0:6], col[:, a:a + 6], ALU.add).then_inc(chain, 1)
                t.wait(chain)
                v.tensor_scalar(bfold[:, 8:10], bfold[:, 0:2], 0.25, None, ALU.mult)
                for wt, name in ((yq, "qnw"), (yk, "cnw"), (yv, "cnw")):
                    for c in range(C2):
                        v.tensor_scalar(wt[:, c, :], wt[:, c, :], cc(name)[:, c:c + 1], None, ALU.mult)
                for s in SLOTS:
                    v.memset(V0[s][:, :, 16:17], 1.0)
                    v.memset(V64[s][:, :, 64:65], 1.0)
                    v.memset(V32[s][:, :, 32:33], 1.0)
                    v.memset(V16[s][:, :, :, 16:17], 1.0)
                    v.memset(KM[s][:, :, :, :], 0.0)
                    m = v.memset(KM4[s][:, :, :, :], 0.0)
                dve.drain().then_inc(m_in[1], 1)
                dve.wait_ge(go, 1)
                with dve.Fori(0, nb // 2) as i:
                    t = Tally(dve)

                    def layernorm(s):
                        v.bn_stats(st6[s][0:T, 0, :], X[s][:, :]).then_inc(vec_done[s], 1)
                        t.wait(vec_done[s])
                        v.bn_aggr(mv[s][0:T, 0, :], st6[s][0:T, 0, :]).then_inc(vec_done[s], 1)
                        t.wait(vec_done[s])
                        v.tensor_scalar(var[s][0:T, 0:1], mv[s][0:T, 0, 1:2], EPS, None, ALU.add).then_inc(ln_var[s], 1)

                    def normalise(s):
                        t.wait(ln_rstd[s])
                        v.tensor_scalar(XN[s][:, :], X[s][:, :], mv[s][0:T, 0, 0:1], rstd[s][0:T, 0:1], ALU.subtract, ALU.mult).then_inc(xn_ready[s], 1)

                    def shift_units(units, evac=None):
                        for u in range(units + (2 if evac else 0)):
                            for s in SLOTS:
                                if u < units:
                                    t.wait(s_psum[s])
                                    sc = bank[s][u % 2][0:T, 0:QW].rearrange("p (h k) -> p h k", h=4)
                                    v.tensor_reduce(mx[s][:, 0:4], sc, AX_X, ALU.max).then_inc(vec_done[s], 1)
                                    if u >= 2:
                                        t.wait(pt_psum[s])
                                    t.wait(vec_done[s])
                                    v.tensor_tensor(P[s][0:T, u % 2, :].rearrange("p (h k) -> p h k", h=4), sc,
                                                    mx[s][:, 0:4].unsqueeze(2).to_broadcast((T, 4, T)), ALU.subtract).then_inc(s_shifted[s], 1)
                            for s in SLOTS:
                                if evac and u >= 2:
                                    evac(s, u - 2)

                    def normalise_o(s, nh, hd, o0_=0):
                        t.wait(o_psum[s])
                        o = bank[s][3][0:T, 0:nh * (hd + 1)].rearrange("p (h d) -> p h d", h=nh)
                        v.reciprocal(rec[s][:, 0:nh], o[:, :, hd]).then_inc(vec_done[s], 1)
                        t.wait(vec_done[s])
                        v.tensor_tensor(ON[s][:, o0_:o0_ + nh * hd].rearrange("p (h d) -> p h d", h=nh), o[:, :, 0:hd],
                                        rec[s][:, 0:nh].unsqueeze(2).to_broadcast((T, nh, hd)), ALU.mult).then_inc(on_ready[s], 1)

                    def residual(s, bk, bias=None):
                        t.wait(y_psum[s])
                        v.tensor_tensor(X[s][:, :], X[s][:, :], bank[s][bk][0:T, 0:D], ALU.add).then_inc(vec_done[s], 1)
                        t.wait(vec_done[s])
                        if bias is not None:
                            v.tensor_tensor(X[s][:, :], X[s][:, :], bias, ALU.add).then_inc(vec_done[s], 1)
                            t.wait(vec_done[s])

                    for s in SLOTS:
                        t.wait(x_in[s], 16)
                        layernorm(s)
                    for s in SLOTS:
                        normalise(s)
                    for s in SLOTS:
                        t.wait(sq_ready[s])
                        v.tensor_reduce(var[s][0:T, 0:20], SQ[s][:, :].rearrange("p (h d) -> p h d", h=20), AX_X, ALU.add).then_inc(vec_done[s], 1)
                        t.wait(vec_done[s])
                        v.tensor_scalar(var[s][0:T, 0:20], var[s][0:T, 0:20], 1.0 / 16, EPS, ALU.mult, ALU.add).then_inc(rms_var[s], 1)
                    for s in SLOTS:
                        t.wait(rms_rstd[s])
                        q3 = QKN[s][:, :].rearrange("p (h d) -> p h d", h=20)
                        v.tensor_tensor(q3, bank[s][0][0:T, 0:320].rearrange("p (h d) -> p h d", h=20),
                                        rstd[s][0:T, 0:20].unsqueeze(2).to_broadcast((T, 20, 16)), ALU.mult).then_inc(vec_done[s], 1)
                        t.wait(vec_done[s])
                        t3 = T2[s][:, :].rearrange("p (h d) -> p h d", h=20)
                        v.tensor_tensor(t3[:, :, 0:8], q3[:, :, 8:16], sin[:, 0:8].unsqueeze(1).to_broadcast((T, 20, 8)), ALU.mult)
                        v.tensor_tensor(t3[:, :, 8:16], q3[:, :, 0:8], sin[:, 8:16].unsqueeze(1).to_broadcast((T, 20, 8)), ALU.mult).then_inc(vec_done[s], 1)
                        t.wait(vec_done[s])
                        v.tensor_tensor(q3, q3, cos.unsqueeze(1).to_broadcast((T, 20, 16)), ALU.mult).then_inc(vec_done[s], 1)
                        t.wait(vec_done[s])
                        v.tensor_tensor(R[s][:, 0:D], QKN[s][:, 0:D], T2[s][:, 0:D], ALU.add)
                        v.tensor_tensor(R[s][:, D:2 * D].rearrange("p (g r d) -> p g r d", g=4, r=4),
                                        q3[:, 16:20, :].unsqueeze(2).to_broadcast((T, 4, 4, 16)),
                                        t3[:, 16:20, :].unsqueeze(2).to_broadcast((T, 4, 4, 16)), ALU.add).then_inc(rope_ready[s], 1)
                    for s in SLOTS:
                        normalise_o(s, H, 16)
                    for s in SLOTS:
                        residual(s, 0)
                        if stop > 1:
                            layernorm(s)

                    if stop > 1:
                        for s in SLOTS:
                            normalise(s)
                        for g in range(2):
                            for s in SLOTS:
                                t.wait(proj_psum[s], 2 if g == 0 else 1)
                                for hh in range(2):
                                    r = slice(64 * hh, 64 * hh + 64)
                                    m = v.tensor_tensor(KM[s][r, 4 * g:4 * g + 4, hh, :], bank[s][g][r, 0:QW].rearrange("p (c q) -> p c q", c=4),
                                                        cc("xbk")[r, 4 * g:4 * g + 4].unsqueeze(2).to_broadcast((64, 4, T)), ALU.add)
                                m.then_inc(proj_vec[s], 1)
                        for g in range(2):
                            for s in SLOTS:
                                t.wait(proj_psum[s], 1)
                                v.scalar_tensor_tensor(out=QT[s][:, 4 * g:4 * g + 4, :], in0=bank[s][(2, 0)[g]][:, 0:QW].rearrange("p (c q) -> p c q", c=4),
                                                       scalar=0.125, in1=bq8[:, 4 * g:4 * g + 4].unsqueeze(2).to_broadcast((128, 4, T)),
                                                       op0=ALU.mult, op1=ALU.add).then_inc(proj_vec[s], 1)
                        for s in SLOTS:
                            t.skip(s_psum[s], 4)
                        shift_units(4, lambda s, u: normalise_o(s, 4, 64, u * D))
                        for s in SLOTS:
                            t.skip(pt_psum[s], 2)
                        for g in range(2):
                            for s in SLOTS:
                                t.wait(ox_psum[s])
                                v.tensor_tensor(OT[s][:, 4 * g:4 * g + 4, :], bank[s][2 + g][:, 0:QW].rearrange("p (c q) -> p c q", c=4),
                                                cc("xbv")[:, 4 * g:4 * g + 4].unsqueeze(2).to_broadcast((128, 4, T)), ALU.add).then_inc(ot_ready[s], 1)
                        for s in SLOTS:
                            residual(s, 0, rr("xbo"))
                            if stop > 2:
                                layernorm(s)

                    if stop > 2:
                        for s in SLOTS:
                            normalise(s)
                        for s in SLOTS:
                            t.wait(ev_ready[s])
                            for k in range(4):
                                v.tensor_scalar(E2[s][:, :, 64 * k:64 * k + 64], ev[s][:, D:2 * D].rearrange("p (r j) -> p j r", j=4),
                                                ident[0:4, k:k + 1], None, ALU.mult)
                                m = v.tensor_scalar(EV[s][:, k, :], ev[s][:, 0:D], ident[0:4, k:k + 1], None, ALU.mult)
                            m.then_inc(ev_ready[s], 1)
                        for s in SLOTS:
                            residual(s, 3, rr("fb2"))
                            if stop > 3:
                                layernorm(s)

                    if stop > 3:
                        for s in SLOTS:
                            normalise(s)
                        for s in SLOTS:
                            t.skip(proj_psum[s], 2)
                            t.wait(proj_psum[s])
                            for hh in range(4):
                                r = slice(32 * hh, 32 * hh + 32)
                                m = v.tensor_copy(KM4[s][r, :, hh, :], bank[s][0][r, 0:C2 * T].rearrange("p (c q) -> p c q", c=C2))
                            m.then_inc(proj_vec[s], 1)
                        if stop > 4:
                            for s in SLOTS:
                                for k in range(KT3):
                                    v.bn_stats(st6[s][0:KP, k, :], CX[s][:, k, :]).then_inc(vec_done[s], 1)
                                t.wait(vec_done[s], KT3)
                                for k in range(KT3):
                                    v.bn_aggr(mv[s][0:KP, k, :], st6[s][0:KP, k, :]).then_inc(vec_done[s], 1)
                                t.wait(vec_done[s], KT3)
                                v.tensor_scalar(var[s][0:KP, 0:KT3], mv[s][0:KP, :, 1], EPS, None, ALU.add).then_inc(ln_var[s], 1)
                            for s in SLOTS:
                                t.wait(ln_rstd[s])
                                for k in range(KT3):
                                    v.tensor_scalar(CX[s][:, k, :], CX[s][:, k, :], mv[s][0:KP, k, 0:1], rstd[s][0:KP, k:k + 1],
                                                    ALU.subtract, ALU.mult).then_inc(cn_ready[s], 1)
                        shift_units(2)
                        for s in SLOTS:
                            normalise_o(s, 8, 32)
                        for s in SLOTS:
                            residual(s, 0)
                            if stop > 4:
                                layernorm(s)

                    if stop > 4:
                        for s in SLOTS:
                            normalise(s)
                        for h in range(H):
                            for s in SLOTS:
                                t.wait(s_psum[s])
                                v.tensor_reduce(mx[s][:, h:h + 1], bank[s][h % 2][0:T, 0:LC], AX_X, ALU.max, negate=True).then_inc(s_shifted[s], 1)
                        for s in SLOTS:
                            normalise_o(s, H, 16)
                        for s in SLOTS:
                            residual(s, 0, rr("ybo"))
                            layernorm(s)
                        for s in SLOTS:
                            normalise(s)
                    dve.drain().then_inc(engines_done, 1)
                    dve.wait_ge(go, i + 2)

            @block.gpsimd
            def _(pool):
                g = nc.gpsimd
                nhalf = sa("nhalf", [128, 20])
                g.memset(nhalf[:, :], -0.5).then_inc(halves_ready, 1)
                pool.wait_ge(halves_ready, 1)
                pool.wait_ge(go, 1)
                with pool.Fori(0, nb // 2) as i:
                    t = Tally(pool)

                    def inverse_root(s, ready, done, rows, n):
                        t.wait(ready[s])
                        g.tensor_tensor(rstd[s][0:rows, 0:n], var[s][0:rows, 0:n], nhalf[0:rows, 0:n], ALU.pow).then_inc(done[s], 1)

                    def mask_heads(s):
                        for c in range(C2):
                            g.tensor_tensor(QM[s][:, c, :, :], QT[s][:, c, :].unsqueeze(1).to_broadcast((128, 8, T)), hm8, ALU.mult).then_inc(masked_ready[s], 1)

                    for s in SLOTS:
                        inverse_root(s, ln_var, ln_rstd, T, 1)
                    for s in SLOTS:
                        inverse_root(s, rms_var, rms_rstd, T, 20)
                    for s in SLOTS:
                        t.wait(qk_copied[s], 2)
                        mask_heads(s)
                    for u in range(4):
                        for s in SLOTS:
                            t.wait(act_done[s])
                            p3 = P[s][0:T, u % 2, :].rearrange("p (h k) -> p h k", h=4)
                            g.tensor_tensor(p3, p3, tri.unsqueeze(1).to_broadcast((T, 4, T)), ALU.mult).then_inc(p_ready[s], 1)
                    if stop > 1:
                        for s in SLOTS:
                            inverse_root(s, ln_var, ln_rstd, T, 1)
                    if stop > 2:
                        for s in SLOTS:
                            inverse_root(s, ln_var, ln_rstd, T, 1)
                    if stop > 3:
                        for s in SLOTS:
                            inverse_root(s, ln_var, ln_rstd, T, 1)
                    if stop > 4:
                        for s in SLOTS:
                            inverse_root(s, ln_var, ln_rstd, KP, 3)
                        for s in SLOTS:
                            inverse_root(s, ln_var, ln_rstd, T, 1)
                        for s in SLOTS:
                            t.wait(qk_copied[s])
                            mask_heads(s)
                        for s in SLOTS:
                            inverse_root(s, ln_var, ln_rstd, T, 1)
                    pool.drain().then_inc(engines_done, 1)
                    pool.wait_ge(go, i + 2)


        routed = sem("routed")
        route_vec = sem("route_vec")
        route_pe = sem("route_pe")
        route_act = sem("route_act")
        route_dma = sem("route_dma")
        added = sem("added")
        gate_shifted, gate_exp = sem("gate_shifted"), sem("gate_exp")
        NI = B * TOPK
        base = nb // 2 + 1
        with ExitStack() as phase:
            def sa(name, shape, dt=F32):
                return phase.enter_context(nc.sbuf_tensor(name, shape, dt))

            def two(name, shape, dt=F32):
                return [sa(f"{name}{s}", shape, dt) for s in SLOTS]

            wexp, rexp = two("wexp", [128, NWE]), two("rexp", [T, NRE])
            gates = sa("gates", [T, NI])
            items = sa("items", [1, 2 * NI + 2], I32)
            rt = sa("rt", [B, NRT])
            lgt, gbt = sa("lgt", [B, E]), sa("gbt", [B, E])
            cmp1, cmp2 = sa("cmp1", [B, E, E]), sa("cmp2", [B, E, E])
            rank, member, gmax, gexp, gsum, gw = (sa("rank", [B, E]), sa("member", [B, E]), sa("gmax", [B, 1]),
                                                  sa("gexp", [B, E]), sa("gsum", [B, 1]), sa("gw", [B, E]))
            tot, pos = sa("tot", [B, E]), sa("pos", [B, E])
            vals = sa("vals", [B, E, 3])
            onehot = sa("onehot", [B, E, NI])
            listf, listi = sa("listf", [3, NI]), sa("listi", [2, NI], I32)
            iota = rt[:, 0:NI]
            below = rt[:, NI:NI + B]
            lower = rt[:, NI + B:NI + B + E * E].rearrange("p (a c) -> p a c", a=E)
            bidx = rt[:, NI + B + E * E:NI + B + E * E + 1 + E]
            onesq = sa("onesq", [B, B])

            X, Z, Y = two("BX", [T, D]), two("BZ", [T, D]), two("BY", [T, D])
            ZN = two("ZN", [T, D])
            XT, ZT, QT, KT = (two("BXT", [128, C2, T]), two("BZT", [128, C2, T]), two("BQT", [128, C2, T]),
                              two("BKT", [128, C2, T]))
            KM = two("BKM", [128, C2, 8, T])
            V16 = two("BV16", [T, H, 17])
            P, PT = two("BP", [T, 2, QW]), two("BPT", [T, 2, QW])
            mx, rec = two("Bmx", [T, 4]), two("Brec", [T, H])
            ON, OT, HT = two("BON", [T, D]), two("BOT", [128, C2, T]), two("BHT", [128, FT, T])
            st6, mv, var, rstd = two("Bst6", [T, 6]), two("Bmv", [T, 2]), two("Bvar", [T, 1]), two("Brstd", [T, 1])
            nhalf = sa("Bnhalf", [T, 1])

            def W(s, name, c):
                a, b = WE[name]
                return wexp[s][:, a:b].rearrange("p (c n) -> p c n", c=c)

            def wc(s, name):
                a, b = WE[name]
                return wexp[s][:, a:b]

            def rr(s, name):
                a, b = RE[name]
                return rexp[s][:, a:b]

            block = phase.enter_context(nc.Block())

            @block.sync
            def _(sp):
                sp.dma_start(lgt[:, :], lg).then_inc(route_dma, 16)
                sp.dma_start(gbt[:, :], gb.to_broadcast((B, E))).then_inc(route_dma, 16)
                sp.wait_ge(routed, 1)
                sp.dma_start(sel[0:1, :], listf[2:3, :]).then_inc(route_dma, 16)
                sp.dma_start(items[0:1, 0:NI], listi[0:1, :]).then_inc(route_dma, 16)
                sp.dma_start(items[0:1, NI + 1:NI + 1 + B], listi[1:2, 0:B]).then_inc(route_dma, 16)
                sp.dma_start(items[0:1, NI + 2 + B:2 * NI + 2], listi[1:2, B:NI]).then_inc(route_dma, 16)
                sp.wait_ge(route_dma, 16 * 6)
                sp.dma_start(gates[:, :], sel[0:1, :].to_broadcast((T, NI))).then_inc(route_dma, 16)
                sp.wait_ge(route_dma, 16 * 7)
                sp.sem_inc(routed, 1)
                with sp.Fori(0, nb) as i:
                    t = Tally(sp)
                    for s in SLOTS:
                        b = sp.value_load(items[0:1, bass.ds(i + s * B, 1)], min_val=0, max_val=B - 1)
                        sp.dma_start(X[s][:, :], xmid[bass.ds(b, 1), :, :].rearrange("a t d -> (a t) d")).then_inc(x_in[s], 16)
                        old = sp.value_load(items[0:1, bass.ds(i + (NI + s * (B + 1)), 1)], min_val=-1, max_val=E - 1)
                        new = sp.value_load(items[0:1, bass.ds(i + (NI + s * (B + 1) + 1), 1)], min_val=0, max_val=E - 1)
                        with sp.If(old != new):
                            sp.dma_start(wexp[s][:, :], we[bass.ds(new, 1), :, :].rearrange("a p n -> (a p) n")).then_inc(c_in[s], 16)
                            sp.dma_start(rexp[s][:, :], re_[bass.ds(new, 1), :].to_broadcast((T, NRE))).then_inc(m_in[s], 16)
                        with sp.Else():
                            sp.sem_inc(c_in[s], 16)
                            sp.sem_inc(m_in[s], 16)
                        sp.nop()
                    t.wait(engines_done, 4)
                    sp.sem_clear(step_sems).then_inc(go, 1)
                sp.wait_ge(added, 16 + 32 * nb)

            @block.tensor
            def _(pe):
                mm = nc.tensor.matmul
                pe.wait_ge(added, 16)
                pe.wait_ge(route_act, 1)
                mm(bank[0][0][0:B, 0:E], below, member[:, :], start=True, stop=True)
                mm(bank[0][1][0:B, 0:E], onesq[:, :], member[:, :], start=True, stop=True).then_inc(route_pe, 1)
                pe.wait_ge(route_act, 2)
                for e in range(E):
                    m = mm(bank[0][2][0:3, 0:NI], vals[:, e, :], onehot[:, e, :], start=(e == 0), stop=(e == E - 1))
                m.then_inc(route_pe, 1)
                pe.wait_ge(routed, 2)
                with pe.Fori(0, nb) as i:
                    t = Tally(pe)

                    def transposes(s, src, bk, ready, done):
                        t.wait(ready[s])
                        for c in range(C2):
                            m = nc.tensor.transpose(bank[s][bk][:, c * T:(c + 1) * T], src[s][:, c * 128:(c + 1) * 128], ident[0:T, 0:T])
                        m.then_inc(done[s], 1)

                    for s in SLOTS:
                        t.wait(x_in[s], 16)
                        for c in range(C2):
                            m = nc.tensor.transpose(bank[s][2][:, c * T:(c + 1) * T], X[s][:, c * 128:(c + 1) * 128], ident[0:T, 0:T])
                        m.then_inc(xt_psum[s], 1)
                    for s in SLOTS:
                        t.wait(xt_ready[s])
                        t.wait(c_in[s], 16)
                        qkv = W(s, "qkv", C2)
                        for bk, n0 in ((1, D), (0, 0)):
                            for m2 in range(C2):
                                for c in range(C2):
                                    m = mm(bank[s][bk][:, m2 * T:(m2 + 1) * T], qkv[:, c, n0 + m2 * 128:n0 + (m2 + 1) * 128],
                                           XT[s][:, c, :], start=(c == 0), stop=(c == 1))
                            m.then_inc(proj_psum[s], 1)
                        for c in range(C2):
                            m = mm(bank[s][3][0:T, 0:D], XT[s][:, c, :], qkv[:, c, 2 * D:3 * D], start=(c == 0), stop=(c == 1))
                        m.then_inc(proj_psum[s], 1)
                    for s in SLOTS:
                        t.wait(proj_act[s], 2)
                    for u in range(6):
                        for s in SLOTS:
                            if u < 4:
                                if u % 2 == 0:
                                    t.wait(masked_ready[s])
                                if u >= 2:
                                    t.wait(s_shifted[s])
                                mm(bank[s][u % 2][0:T, 0:QW], QT[s][:, u // 2, :], KM[s][:, u // 2, 4 * (u % 2):4 * (u % 2) + 4, :],
                                   start=True, stop=True).then_inc(s_psum[s], 1)
                        for s in SLOTS:
                            if u >= 2:
                                v = u - 2
                                t.wait(pt_ready[s])
                                for h in range(4):
                                    m = mm(bank[s][3][0:T, 17 * (4 * v + h):17 * (4 * v + h) + 17], PT[s][:, v % 2, h * T:(h + 1) * T],
                                           V16[s][:, 4 * v + h, :], start=True, stop=True)
                                m.then_inc(pv_done[s] if v < 3 else o_psum[s], 1)
                        for s in SLOTS:
                            if 1 <= u < 5:
                                t.wait(p_ready[s])
                                for h in range(4):
                                    m = nc.tensor.transpose(bank[s][2][0:T, h * T:(h + 1) * T], P[s][:, (u - 1) % 2, h * T:(h + 1) * T], ident[0:T, 0:T])
                                m.then_inc(pt_psum[s], 1)
                    for s in SLOTS:
                        transposes(s, ON, 2, on_ready, ot_psum)
                    for s in SLOTS:
                        t.wait(ot_ready[s])
                        for c in range(C2):
                            m = mm(bank[s][0][0:T, 0:D], OT[s][:, c, :], W(s, "o", C2)[:, c, :], start=(c == 0), stop=(c == 1))
                        m.then_inc(y_psum[s], 1)
                    for s in SLOTS:
                        transposes(s, Z, 2, xn_ready, xt_psum)
                    for s in SLOTS:
                        t.wait(xt_ready[s])
                        for g in range(2):
                            for j in range(4):
                                mt = 4 * g + j
                                for c in range(C2):
                                    m = mm(bank[s][g][:, j * T:(j + 1) * T], W(s, "l1", C2)[:, c, mt * 128:(mt + 1) * 128], ZT[s][:, c, :],
                                           start=(c == 0), stop=(c == 1))
                            m.then_inc(h_psum[s], 1)
                    for s in SLOTS:
                        for g in range(2):
                            t.wait(h_ready[s])
                            for j in range(4):
                                mt = 4 * g + j
                                m = mm(bank[s][3][0:T, 0:D], HT[s][:, mt, :], W(s, "l2", FT)[:, mt, :], start=(mt == 0), stop=(mt == FT - 1))
                        m.then_inc(y_psum[s], 1)
                    pe.drain().then_inc(engines_done, 1)
                    pe.wait_ge(go, i + (base + 1))

            @block.scalar
            def _(act):
                A = nc.scalar.activation
                act.wait_ge(gate_shifted, 1)
                A(gexp[:, :], gw[:, :], ACT.Exp, accum_out=gsum[:, :]).then_inc(gate_exp, 1)
                act.wait_ge(routed, 2)
                with act.Fori(0, nb) as i:
                    t = Tally(act)

                    def copy2(dst, s, bk, ready, done):
                        t.wait(ready[s])
                        A(dst[s][:, :, :], bank[s][bk][:, 0:C2 * T].rearrange("p (c q) -> p c q", c=C2), ACT.Copy).then_inc(done[s], 1)

                    for s in SLOTS:
                        copy2(XT, s, 2, xt_psum, xt_ready)
                    for s in SLOTS:
                        for dst, bk, name in ((KT, 1, "bk"), (QT, 0, "bq")):
                            t.wait(proj_psum[s])
                            for m2 in range(C2):
                                m = A(dst[s][:, m2, :], bank[s][bk][:, m2 * T:(m2 + 1) * T], ACT.Identity, bias=wc(s, name)[:, m2:m2 + 1])
                                if bk == 1:
                                    m.then_inc(qk_copied[s], 1)
                            if bk == 0:
                                m.then_inc(proj_act[s], 1)
                        t.wait(proj_psum[s])
                        A(V16[s][:, :, 0:16], bank[s][3][0:T, 0:D].rearrange("p (h d) -> p h d", h=H), ACT.Copy).then_inc(proj_act[s], 1)
                    for u in range(5):
                        for s in SLOTS:
                            if u < 4:
                                t.wait(s_shifted[s])
                                A(P[s][:, u % 2, :], P[s][:, u % 2, :], ACT.Exp).then_inc(p_ready[s], 1)
                        for s in SLOTS:
                            if u > 0:
                                v = u - 1
                                t.wait(pt_psum[s])
                                if v >= 2:
                                    t.wait(pv_done[s])
                                A(PT[s][:, v % 2, :], bank[s][2][0:T, 0:QW], ACT.Copy).then_inc(pt_ready[s], 1)
                    for s in SLOTS:
                        t.wait(ot_psum[s])
                        for m2 in range(C2):
                            m = A(OT[s][:, m2, :], bank[s][2][:, m2 * T:(m2 + 1) * T], ACT.Identity, bias=wc(s, "bv")[:, m2:m2 + 1])
                        m.then_inc(ot_ready[s], 1)
                    for s in SLOTS:
                        copy2(ZT, s, 2, xt_psum, xt_ready)
                    for s in SLOTS:
                        for g in range(2):
                            t.wait(h_psum[s])
                            for j in range(4):
                                mt = 4 * g + j
                                m = A(HT[s][:, mt, :], bank[s][g][:, j * T:(j + 1) * T], ACT.Relu, bias=wc(s, "b1")[:, mt:mt + 1])
                            m.then_inc(h_ready[s], 1)
                    act.drain().then_inc(engines_done, 1)
                    act.wait_ge(go, i + (base + 1))

            @block.vector
            def _(dve):
                v = nc.vector
                t = Tally(dve)
                chain = route_vec

                def step(ins):
                    ins.then_inc(chain, 1)
                    t.wait(chain)

                dve.wait_ge(route_dma, 16 * 2)
                dve.wait_ge(added, 16)
                v.memset(items[:, NI:NI + 1], -1)
                v.memset(items[:, NI + 1 + B:NI + 2 + B], -1)
                for s in SLOTS:
                    v.memset(V16[s][:, :, 16:17], 1.0)
                v.memset(onesq[:, :], 1.0)
                v.tensor_copy(vals[:, :, 1], bidx[:, 1:1 + E])
                v.tensor_copy(vals[:, :, 0], bidx[:, 0:1].to_broadcast((B, E)))
                step(v.tensor_tensor(lgt[:, :], lgt[:, :], gbt[:, :], ALU.add))
                mine = lgt[:, :].unsqueeze(2).to_broadcast((B, E, E))
                other = lgt[:, :].unsqueeze(1).to_broadcast((B, E, E))
                v.tensor_tensor(cmp1[:, :, :], other, mine, ALU.is_gt)
                step(v.tensor_tensor(cmp2[:, :, :], other, mine, ALU.is_equal))
                step(v.tensor_tensor(cmp2[:, :, :], cmp2[:, :, :], lower, ALU.mult))
                step(v.tensor_tensor(cmp1[:, :, :], cmp1[:, :, :], cmp2[:, :, :], ALU.add))
                step(v.tensor_reduce(rank[:, :], cmp1[:, :, :], AX_X, ALU.add))
                v.tensor_reduce(gmax[:, :], lgt[:, :], AX_X, ALU.max, negate=True)
                v.tensor_scalar(member[:, :], rank[:, :], TOPK - 0.5, None, ALU.is_lt).then_inc(route_act, 1)
                dve.wait_ge(route_act, 1)
                v.tensor_scalar(gw[:, :], lgt[:, :], gmax[:, :], None, ALU.add).then_inc(gate_shifted, 1)
                dve.wait_ge(route_pe, 1)
                step(v.tensor_copy(tot[:, :], bank[0][1][0:B, 0:E]))
                step(v.tensor_copy(pos[:, :], bank[0][0][0:B, 0:E]))
                for e in range(1, E):
                    step(v.tensor_scalar(pos[:, e:E], pos[:, e:E], tot[:, e - 1:e], None, ALU.add))
                for e in range(E):
                    step(v.tensor_scalar(onehot[:, e, :], iota, pos[:, e:e + 1], member[:, e:e + 1], ALU.is_equal, ALU.mult))
                dve.wait_ge(gate_exp, 1)
                step(v.reciprocal(gsum[:, :], gsum[:, :]))
                v.tensor_scalar(vals[:, :, 2], gexp[:, :], gsum[:, :], None, ALU.mult).then_inc(route_act, 1)
                dve.wait_ge(route_pe, 2)
                step(v.tensor_copy(listf[:, :], bank[0][2][0:3, 0:NI]))
                v.tensor_copy(listi[:, :], listf[0:2, :]).then_inc(routed, 1)
                dve.wait_ge(routed, 2)
                with dve.Fori(0, nb) as i:
                    t = Tally(dve)
                    def layernorm(s, src):
                        v.bn_stats(st6[s][:, :], src[s][:, :]).then_inc(vec_done[s], 1)
                        t.wait(vec_done[s])
                        v.bn_aggr(mv[s][:, :], st6[s][:, :]).then_inc(vec_done[s], 1)
                        t.wait(vec_done[s])
                        v.tensor_scalar(var[s][:, :], mv[s][:, 1:2], EPS, None, ALU.add).then_inc(ln_var[s], 1)

                    def normalise(s, src, dst, wname, bname, ready):
                        t.wait(ln_rstd[s])
                        v.tensor_scalar(ZN[s][:, :], src[s][:, :], mv[s][:, 0:1], rstd[s][:, :], ALU.subtract, ALU.mult).then_inc(vec_done[s], 1)
                        t.wait(vec_done[s])
                        v.tensor_tensor(ZN[s][:, :], ZN[s][:, :], rr(s, wname), ALU.mult).then_inc(vec_done[s], 1)
                        t.wait(vec_done[s])
                        v.tensor_tensor(dst[s][:, :], ZN[s][:, :], rr(s, bname), ALU.add).then_inc(ready[s], 1)

                    def add_psum(s, dst, src, bk, bname):
                        t.wait(y_psum[s])
                        v.tensor_tensor(dst[s][:, :], src[s][:, :], bank[s][bk][0:T, 0:D], ALU.add).then_inc(vec_done[s], 1)
                        t.wait(vec_done[s])
                        v.tensor_tensor(dst[s][:, :], dst[s][:, :], rr(s, bname), ALU.add).then_inc(vec_done[s], 1)
                        t.wait(vec_done[s])

                    for s in SLOTS:
                        t.wait(x_in[s], 16)
                        t.wait(m_in[s], 16)
                    for u in range(4):
                        for s in SLOTS:
                            t.wait(s_psum[s])
                            sc = bank[s][u % 2][0:T, 0:QW].rearrange("p (h k) -> p h k", h=4)
                            v.tensor_reduce(mx[s][:, :], sc, AX_X, ALU.max).then_inc(vec_done[s], 1)
                            if u >= 2:
                                t.wait(pt_psum[s])
                            t.wait(vec_done[s])
                            v.tensor_tensor(P[s][:, u % 2, :].rearrange("p (h k) -> p h k", h=4), sc,
                                            mx[s][:, :].unsqueeze(2).to_broadcast((T, 4, T)), ALU.subtract).then_inc(s_shifted[s], 1)
                    for s in SLOTS:
                        t.wait(o_psum[s])
                        o = bank[s][3][0:T, 0:H * 17].rearrange("p (h d) -> p h d", h=H)
                        v.reciprocal(rec[s][:, :], o[:, :, 16]).then_inc(vec_done[s], 1)
                        t.wait(vec_done[s])
                        v.tensor_tensor(ON[s][:, :].rearrange("p (h d) -> p h d", h=H), o[:, :, 0:16],
                                        rec[s][:, :].unsqueeze(2).to_broadcast((T, H, 16)), ALU.mult).then_inc(on_ready[s], 1)
                    for s in SLOTS:
                        add_psum(s, X, X, 0, "ob")
                        layernorm(s, X)
                    for s in SLOTS:
                        normalise(s, X, Z, "n1w", "n1b", xn_ready)
                    for s in SLOTS:
                        add_psum(s, X, Z, 3, "l2b")
                        layernorm(s, X)
                    for s in SLOTS:
                        normalise(s, X, Z, "n2w", "n2b", vec_done)
                        t.wait(vec_done[s])
                        if s == 0:
                            dve.wait_ge(added, i * 32 + 16)
                        v.tensor_scalar(Y[s][:, :], Z[s][:, :], gates[:, bass.ds(i + s * B, 1)], None, ALU.mult).then_inc(x_ready[s], 1)
                    dve.drain().then_inc(engines_done, 1)
                    dve.wait_ge(go, i + (base + 1))

            @block.gpsimd
            def _(pool):
                g = nc.gpsimd
                g.memset(nhalf[:, :], -0.5).then_inc(halves_ready, 1)
                pool.wait_ge(halves_ready, 2)
                g.dma_start(rt[:, :], rtc).then_inc(added, 16)
                pool.wait_ge(routed, 2)
                with pool.Fori(0, nb) as i:
                    t = Tally(pool)

                    def inverse_root(s):
                        t.wait(ln_var[s])
                        g.tensor_tensor(rstd[s][:, :], var[s][:, :], nhalf[:, :], ALU.pow).then_inc(ln_rstd[s], 1)

                    batches = [pool.value_load(items[0:1, bass.ds(i + s * B, 1)], min_val=0, max_val=B - 1) for s in SLOTS]
                    for c in range(C2):
                        for s in SLOTS:
                            t.wait(qk_copied[s])
                            g.tensor_tensor(KM[s][:, c, :, :], KT[s][:, c, :].unsqueeze(1).to_broadcast((128, 8, T)), hm8q, ALU.mult).then_inc(masked_ready[s], 1)
                    for s in SLOTS:
                        inverse_root(s)
                    for s in SLOTS:
                        inverse_root(s)
                    for s in SLOTS:
                        t.wait(x_ready[s])
                        pool.wait_ge(added, i * 32 + 16 * (s + 1))
                        g.dma_start(out[bass.ds(batches[s], 1), :, :].rearrange("a t d -> (a t) d"), Y[s][:, :],
                                    accum_op=ALU.add).then_inc(added, 16)
                    pool.drain().then_inc(engines_done, 1)
                    pool.wait_ge(go, i + (base + 1))




def _chunks(a):
    import numpy as np
    n = a.shape[0] // 128
    return np.ascontiguousarray(a.reshape(n, 128, -1).transpose(1, 0, 2).reshape(128, -1))


def _cols(v):
    import numpy as np
    return np.ascontiguousarray(v.reshape(-1, 128).T)


def _pack(i):
    import numpy as np
    f = {k: np.asarray(v) for k, v in i.items()}
    cat = np.concatenate
    rep = lambda a, t: cat([a[:, t * 32:(t + 1) * 32]] * 4, 1)
    kd = f["L1_attn_wk_down"]
    wa = {"qkv0": cat([f["L0_attn_w_q"], f["L0_attn_w_k"], f["L0_attn_w_v"]], 1), "o0": f["L0_attn_w_o"],
          "xq": f["L0_xattn_Wq"], "xk": f["L0_xattn_Wk"], "xv": f["L0_xattn_Wv"], "xo": f["L0_xattn_Wo"],
          "f1": f["L0_ffn_W1"].T, "f2": f["L0_ffn_W2"].T, "k1": cat([rep(kd, 0), rep(kd, 1)], 1),
          "v1": f["L1_attn_wv_down"], "yq": f["L1_xattn_Wq"].T, "yk": f["L1_xattn_Wk"].T, "yv": f["L1_xattn_Wv"].T,
          "yo": f["L1_xattn_Wo"].T, "gate": f["L1_ffn_gate_w"].T}
    wa = cat([_chunks(wa[n]) for n, _ in WA_PARTS], 1)
    ca = {"xbq": f["L0_xattn_bq"], "xbk": f["L0_xattn_bk"], "xbv": f["L0_xattn_bv"], "fb1": f["L0_ffn_b1"],
          "qnw": f["L1_xattn_qn_w"], "qnb": f["L1_xattn_qn_b"], "cnw": f["L1_xattn_cn_w"], "cnb": f["L1_xattn_cn_b"],
          "ybq": f["L1_xattn_bq"], "ybk": f["L1_xattn_bk"], "ybv": f["L1_xattn_bv"],
          "scale": np.broadcast_to(f["L0_ffn_scale"], (128,))}
    ca = cat([_cols(ca[n]) for n, _ in CA_PARTS], 1)
    ra = cat([f["L0_xattn_bo"], f["L0_ffn_b2"], f["L1_xattn_bo"]])[None]
    wqt = f["L1_attn_wq"].reshape(D, 8, 128).transpose(2, 1, 0)
    wo = f["L1_attn_wo"].reshape(8, 128, D).transpose(1, 0, 2)
    up = [f["L1_attn_wk_up"].T, f["L1_attn_wv_up"].T]
    for p in range(4):
        up += [wqt[:, 2 * p], wqt[:, 2 * p + 1], wo[:, 2 * p], wo[:, 2 * p + 1]]
    up = cat(up, 1)
    qkvb = f["L1_ffn_in_proj_b"]
    we = [cat([_chunks(f["L1_ffn_in_proj_w"][e].T), _chunks(f["L1_ffn_out_proj_w"][e].T), _chunks(f["L1_ffn_lin1_w"][e].T),
               _chunks(f["L1_ffn_lin2_w"][e].T), _cols(qkvb[e]), _cols(f["L1_ffn_lin1_b"][e])], 1) for e in range(E)]
    re_ = cat([f["L1_ffn_" + n] for n in ("out_proj_b", "ln1_w", "ln1_b", "lin2_b", "ln2_w", "ln2_b")], 1)
    q, d = np.arange(T, dtype=np.float32), np.arange(0, 16, 2, dtype=np.float32)
    inv = (np.float32(1.0) / np.float32(10000.0) ** (d / np.float32(16))).astype(np.float32)
    fr = (q[:, None] * inv[None, :]).astype(np.float32)
    kc = np.zeros((128, NKC), np.float32)
    kc[:, KC["ident"][0]:KC["ident"][1]] = np.eye(128)
    kc[:, KC["hm8"][0]:KC["hm8"][1]] = np.repeat(np.arange(128)[:, None] // 16 == np.arange(8)[None], T, axis=1)
    kc[:, KC["hm8q"][0]:KC["hm8q"][1]] = 0.25 * kc[:, KC["hm8"][0]:KC["hm8"][1]]
    kc[0:T, KC["tri"][0]:KC["tri"][1]] = np.triu(np.ones((T, T)))
    kc[0:T, KC["cos"][0]:KC["cos"][1]] = np.tile(np.cos(fr), (1, 2))
    kc[0:T, KC["sin"][0]:KC["sin"][1]] = cat([-np.sin(fr), np.sin(fr)], 1)
    kc[:, KC["ones"][0]:KC["ones"][1]] = 1.0
    kb = np.zeros((T, T + QW + T), np.float32)
    kb[:, 0:T] = np.eye(T)
    kb[:, T:T + QW] = np.tile(np.triu(np.full((T, T), NEG), 1), (1, 4))
    kb[:, T + QW:] = 1.0
    j = np.arange(B)
    rtc = cat([np.broadcast_to(np.arange(2 * B), (B, 2 * B)), j[:, None] < j[None], np.broadcast_to(np.tril(np.ones((E, E)), -1).reshape(1, -1), (B, E * E)),
               j[:, None], np.broadcast_to(np.arange(E), (B, E))], 1).astype(np.float32)
    x, c = f["x"], f["ctx_1024"]
    return {"x": x, "ctx": c, "mask": f["mask_BxS2_bk0"].astype(np.int32), "wa": wa, "ca": ca, "ra": ra, "up": up,
            "we": np.stack(we), "re": re_, "gb": f["L1_ffn_gate_b"][None], "kc": kc, "rtc": rtc, "kb": kb}


def _program(nc, arrays, stop=9, nb=B):
    a = {n: nc.dram_tensor("in_" + n, v.shape, mybir.dt.from_np(v.dtype), kind="ExternalInput").ap() for n, v in arrays.items()}
    out = nc.dram_tensor("out", (B, T, D), F32, kind="ExternalOutput").ap()
    xmid = nc.dram_tensor("xmid", (B, T, D), F32).ap()
    lg = nc.dram_tensor("lg", (B, E), F32).ap()
    mrow = nc.dram_tensor("mrow", (B, LC), BF16).ap()
    sel = nc.dram_tensor("sel", (4, B * TOPK), F32).ap()
    build(nc, a["x"], a["ctx"], a["mask"], a["wa"], a["ca"], a["ra"], a["up"], a["we"], a["re"], a["gb"], a["kc"], a["kb"], a["rtc"],
          out, xmid, lg, mrow, sel, stop, nb)


def kernel(**inputs):
    import numpy as np
    import concourse.bacc as bacc
    from concourse.bass_utils import run_bass_kernel_spmd

    arrays = {n: np.ascontiguousarray(v) for n, v in _pack(inputs).items()}
    nc = bacc.Bacc("TRN2", target_bir_lowering=False, num_devices=1)
    _program(nc, arrays)
    r = run_bass_kernel_spmd(nc, [{"in_" + n: v for n, v in arrays.items()}], core_ids=[0])
    return r.results[0]["out"]
```

```python
from contextlib import ExitStack

import concourse.bass as bass
from concourse import mybir

F32 = mybir.dt.float32
BF16 = mybir.dt.bfloat16
U32 = mybir.dt.uint32
I32 = mybir.dt.int32
ALU = mybir.AluOpType
ACT = mybir.ActivationFunctionType
AX_X = mybir.AxisListType.X

B, T, D = 32, 112, 256
LC, KT3, KP = 375, 3, 125
C2 = D // 128
H = 16
EPS = 1e-5
NEG = -1e30
CAP = 50.0
E, TOPK, DFF = 4, 2, 1024
FT = DFF // 128
QW = 4 * T

WA_PARTS = [("qkv0", C2 * 384), ("o0", C2 * D), ("xq", C2 * DFF), ("xk", C2 * DFF), ("xv", C2 * DFF), ("xo", FT * D),
            ("f1", C2 * DFF), ("f2", FT * D), ("k1", C2 * D), ("v1", C2 * 64), ("yq", C2 * D), ("yk", C2 * D),
            ("yv", C2 * D), ("yo", C2 * D), ("gate", C2 * E)]
CA_PARTS = [("xbq", FT), ("xbk", FT), ("xbv", FT), ("fb1", FT), ("qnw", C2), ("qnb", C2), ("cnw", C2), ("cnb", C2),
            ("ybq", C2), ("ybk", C2), ("ybv", C2), ("scale", 1)]
RA_PARTS = [("xbo", D), ("fb2", D), ("ybo", D)]
WE_PARTS = [("qkv", C2 * 3 * D), ("bq", C2), ("bk", C2), ("bv", C2), ("b1", FT), ("n1w", C2), ("n1b", C2),
            ("o", C2 * D), ("l1", C2 * DFF), ("l2", FT * D)]
RE_PARTS = [("ob", D), ("n1w", D), ("n1b", D), ("l2b", D), ("n2w", D), ("n2b", D)]
K_PARTS = [("ident", 128), ("hm8", 8 * T), ("tri", T), ("cos", 16), ("sin", 16), ("ones", 1)]


def offsets(parts):
    at, out = 0, {}
    for name, w in parts:
        out[name] = (at, at + w)
        at += w
    return out, at


WA, NWA = offsets(WA_PARTS)
CA, NCA = offsets(CA_PARTS)
RA, NRA = offsets(RA_PARTS)
WE, NWE = offsets(WE_PARTS)
RE, NRE = offsets(RE_PARTS)
KC, NKC = offsets(K_PARTS)
NRT = 2 * B + B + E * E + 1 + E
SLOTS = (0, 1)
BEATS_A, BEATS_B = 74, 26


class Tally:

    def __init__(self, eng):
        self.eng, self.seen = eng, {}

    def wait(self, sem, n=1):
        self.seen[sem.num] = self.seen.get(sem.num, 0) + n
        self.eng.wait_ge(sem, self.seen[sem.num])

    def skip(self, sem, n):
        self.seen[sem.num] = self.seen.get(sem.num, 0) + n


class Place:

    def __init__(self, n, last=False):
        self.n, self.last = n, last


def run_slots(eng, count, batch, beats):
    half = beats // 2
    at = Place([0, 0])

    def start(s):
        program = batch(s, at)
        return [program, next(program)]

    def work(run, beat):
        while run[1] <= beat:
            run[1] = next(run[0], beats)

    other = start(1)
    for beat in range(half):
        work(other, beat)
    with eng.Fori(0, count - 1) as i:
        at.n = [i, i]
        one = start(0)
        for beat in range(beats):
            work(one, beat)
            if beat < beats - half:
                work(other, beat + half)
            else:
                if beat == beats - half:
                    at.n = [i, i + 1]
                    other = start(1)
                work(other, beat - (beats - half))
    at.n, at.last = [count - 1, count - 1], True
    one = start(0)
    for beat in range(beats):
        work(one, beat)
        if beat < beats - half:
            work(other, beat + half)


def build(nc, x, ctx, mask, wa, ca, ra, up, we, re_, gb, kc, kb, rtc, out, xmid, lg, mrow, sel):
    with ExitStack() as es:
        def sb(name, shape, dt=F32):
            return es.enter_context(nc.sbuf_tensor(name, shape, dt))

        def sem(name):
            return es.enter_context(nc.semaphore(name))

        def pair(name):
            return [sem(f"{name}_{s}") for s in SLOTS]

        bank = [[es.enter_context(nc.psum_tensor(f"bank{s}{b}", [128, 512], F32)) for b in range(4)] for s in SLOTS]
        const = sb("const", [128, NKC])
        constb = sb("constb", [T, T + QW + T], BF16)
        ident = const[:, KC["ident"][0]:KC["ident"][1]]
        hm8 = const[:, KC["hm8"][0]:KC["hm8"][1]].rearrange("p (h q) -> p h q", h=8)
        tri = const[0:T, KC["tri"][0]:KC["tri"][1]]
        cos = const[0:T, KC["cos"][0]:KC["cos"][1]]
        sin = const[0:T, KC["sin"][0]:KC["sin"][1]]
        identb, causalb, onesb = constb[:, 0:T], constb[:, T:T + QW], constb[0:1, T + QW:T + QW + T]
        half = B // 2

        loaded, prep, prep_dma = sem("loaded"), sem("prep"), sem("prep_dma")
        mask_ready, all_prepared, halves_ready, prep_vec = sem("mask_ready"), sem("all_prepared"), sem("halves_ready"), sem("prep_vec")
        go = pair("go")
        names = ("started x_in c_in m_in x_out lg_out xn_ready xt_psum xt_ready "
                 "qkv_psum sq_ready rms_var rms_rstd rope_ready qk_psum qk_copied masked_ready tanh_ready exp_ready "
                 "ct_psum ct_ready kx_psum kx_read vx_psum vx_read qx_psum qx_read cn_var cn_rstd cn_ready "
                 "kp_psum kp_read vp_psum vp_read yq_psum la_psum la_vec la_act "
                 "s_psum s_shifted p_ready pt_psum pt_ready pv_done o_psum on_ready ot_psum ot_ready ox_psum y_psum "
                 "sel_psum ev_ready ew_ready g_psum g_ready h_psum h_ready mean_psum mean_ready logit_psum logit_ready "
                 "m_taken late_in ln_var last_started ln_rstd vec_done y_ready y_taken").split()
        batch_sems = [[sem(f"{name}_{s}") for name in names] for s in SLOTS]
        (started, x_in, c_in, m_in, x_out, lg_out, xn_ready, xt_psum, xt_ready,
         qkv_psum, sq_ready, rms_var, rms_rstd, rope_ready, qk_psum, qk_copied, masked_ready, tanh_ready, exp_ready,
         ct_psum, ct_ready, kx_psum, kx_read, vx_psum, vx_read, qx_psum, qx_read, cn_var, cn_rstd, cn_ready,
         kp_psum, kp_read, vp_psum, vp_read, yq_psum, la_psum, la_vec, la_act,
         s_psum, s_shifted, p_ready, pt_psum, pt_ready, pv_done, o_psum, on_ready, ot_psum, ot_ready, ox_psum, y_psum,
         sel_psum, ev_ready, ew_ready, g_psum, g_ready, h_psum, h_ready, mean_psum, mean_ready, logit_psum,
         logit_ready, m_taken, late_in, ln_var, last_started, ln_rstd, vec_done, y_ready, y_taken) = zip(*batch_sems)
        slot_sems = [range(q[0].num, q[-1].num + 1) for q in batch_sems]
        first_sems = [range(batch_sems[s][0].num, ln_var[s].num) for s in SLOTS]
        last_sems = [range(ln_var[s].num, y_taken[s].num + 1) for s in SLOTS]

        with ExitStack() as phase:
            def sa(name, shape, dt=F32):
                return phase.enter_context(nc.sbuf_tensor(name, shape, dt))

            def two(name, shape, dt=F32):
                return [sa(f"{name}{s}", shape, dt) for s in SLOTS]

            w = sa("wa_sb", [128, NWA])
            col = sa("ca_sb", [128, NCA])
            row = sa("ra_sb", [T, NRA])
            wqa = sa("wqa", [128, C2, D])
            woa = sa("woa", [128, C2, D])
            bfold = sa("bfold", [128, 16])
            bq8 = sa("bq8", [128, FT])
            mwords = sa("mwords", [B, LC], I32)
            mfl = sa("mfl", [B, LC])
            mall = sa("mall", [B, 1])
            mneg = sa("mneg", [B, LC], BF16)

            XIN = two("XIN", [T, D])
            X, XN, XT = two("X", [T, D]), two("XN", [T, D]), two("XT", [128, C2, T])
            CX = two("CX", [KP, KT3, D])
            CT = two("CT", [128, C2, LC])
            MR = two("MR", [1, LC], BF16)
            st6, mv, var, rstd = (two("st6", [128, 1, 6]), two("mv", [128, 1, 2]), two("var", [128, 20]),
                                  two("rstd", [128, 20]))
            cst6, cmv, cvar, crstd = (two("cst6", [KP, KT3, 6]), two("cmv", [KP, KT3, 2]), two("cvar", [KP, KT3]),
                                      two("crstd", [KP, KT3]))
            SQ, QKN = two("SQ", [T, 320]), two("QKN", [T, 320])
            T2 = SQ
            QT = two("QT", [128, FT, T])
            KT = two("KT", [128, C2, LC])
            QM = two("QM", [128, C2, 8, T])
            KM = two("KM", [128, FT, 2, T])
            KM4 = two("KM4", [128, C2, 4, T])
            V0 = two("V0", [T, 4, 17])
            V64 = two("V64", [T, H, 65])
            V32 = two("V32", [T, 2, 33])
            V16 = two("V16", [KP, KT3, H, 17])
            P, PT = two("P", [128, 2, QW]), two("PT", [128, 2, QW])
            P4 = [[P[s][0:T, 0, :], P[s][0:T, 1, :], PT[s][0:T, 0, :], PT[s][0:T, 1, :]] for s in SLOTS]
            mx = two("mx", [T, H])
            rec = two("rec", [T, H])
            ON = two("ON", [T, DFF])
            R = [ON[s][:, 2 * D:4 * D] for s in SLOTS]
            OT = two("OT", [128, FT, T])
            ev = [P[s][0:4, :, :].rearrange("p u n -> p (u n)")[:, 0:2 * D] for s in SLOTS]
            EV = [QM[s][0:4, :, :, :].rearrange("p c h q -> p (c h q)")[:, 0:4 * D].rearrange("p (k n) -> p k n", k=4) for s in SLOTS]
            E2 = [ON[s][0:4, :].rearrange("p (k n) -> p k n", k=4) for s in SLOTS]
            GS, G2 = two("GS", [4, T]), two("G2", [4, 4, T])
            xbar, lrow = two("xbar", [128, C2]), two("lrow", [1, E])
            upw = [QM[0][:, :, :, :].rearrange("p c h q -> p (c h q)")[:, 0:1024], QM[1][:, :, :, :].rearrange("p c h q -> p (c h q)")[:, 768:1792],
                   KM[0][:, :, :, :].rearrange("p c h q -> p (c h q)")[:, 0:1024], KM[1][:, :, :, :].rearrange("p c h q -> p (c h q)")[:, 0:1024]]
            upc = sa("upc", [128, 64])
            kbw = QM[1][0:T, :, :, :].rearrange("p c h q -> p (c h q)")[:, 0:T + QW + T]

            def W(name, c):
                a, b = WA[name]
                return w[:, a:b].rearrange("p (c n) -> p c n", c=c)

            def cc(name):
                a, b = CA[name]
                return col[:, a:b]

            def rr(name):
                a, b = RA[name]
                return row[:, a:b]

            qkv0, o0, xq, xk, xv, xo = W("qkv0", C2), W("o0", C2), W("xq", C2), W("xk", C2), W("xv", C2), W("xo", FT)
            f1, f2, k1, v1, gate = W("f1", C2), W("f2", FT), W("k1", C2), W("v1", C2), W("gate", C2)
            yq, yk, yv, yo = W("yq", C2), W("yk", C2), W("yv", C2), W("yo", C2)

            block = phase.enter_context(nc.Block())

            @block.sync
            def _(sp):
                sp.dma_start(upc[:, :], up[:, 0:64]).then_inc(prep_dma, 16)
                for part in range(4):
                    a = 64 + part * 1024
                    sp.dma_start(upw[part], up[:, a:a + 1024]).then_inc(prep_dma, 16)
                for dst, src in ((const[:, :], kc), (kbw, kb), (col[:, :], ca), (mwords[:, :], mask), (w[:, :], wa),
                                 (row[:, :], ra.to_broadcast((T, NRA)))):
                    sp.dma_start(dst, src).then_inc(loaded, 16)
                for s in SLOTS:
                    sp.dma_start(XIN[s][:, :], x[s * half, :, :]).then_inc(x_in[s], 16)
                sp.wait_ge(mask_ready, 1)
                sp.dma_start(mrow, mneg[:, :]).then_inc(loaded, 16)
                sp.wait_ge(loaded, 7 * 16)
                sp.wait_ge(all_prepared, 1)
                for s in SLOTS:
                    sp.wait_ge(x_in[s], 16)
                    sp.sem_clear(slot_sems[s]).then_inc(go[s], 1)

                def batch(s, at):
                    t = Tally(sp)
                    yield 0
                    b = at.n[s] + s * half
                    sp.dma_start(CX[s][:, :, :], ctx[bass.ds(b, 1), :, :].rearrange("a (t p) d -> p (a t) d", p=KP)).then_inc(c_in[s], 16)
                    sp.dma_start(MR[s][:, :], mrow[bass.ds(b, 1), :]).then_inc(m_in[s], 16)
                    yield 40
                    more = not at.last
                    if more:
                        t.wait(ln_var[s], 2)
                        sp.dma_start(XIN[s][:, :], x[bass.ds(at.n[s] + (s * half + 1), 1), :, :].rearrange("a t d -> (a t) d")).then_inc(x_in[s], 16)
                    yield 72
                    b = at.n[s] + s * half
                    t.wait(xn_ready[s], 6)
                    sp.dma_start(out[bass.ds(b, 1), :, :].rearrange("a t d -> (a t) d"), X[s][:, :]).then_inc(x_out[s], 16)
                    sp.dma_start(xmid[bass.ds(b, 1), :, :].rearrange("a t d -> (a t) d"), XN[s][:, :]).then_inc(x_out[s], 16)
                    yield 72
                    t.wait(logit_ready[s])
                    sp.dma_start(lg[bass.ds(b, 1), :], lrow[s][:, :]).then_inc(lg_out[s], 16)
                    t.wait(x_out[s], 32)
                    t.wait(lg_out[s], 16)
                    if more:
                        t.wait(x_in[s], 16)
                    sp.sem_clear(slot_sems[s]).then_inc(go[s], 1)
                run_slots(sp, half, batch, BEATS_A)
                for s in SLOTS:
                    sp.wait_ge(go[s], half + 1)

            @block.tensor
            def _(pe):
                mm, transpose = nc.tensor.matmul, nc.tensor.transpose
                pe.wait_ge(prep_dma, 16 * 5)
                for part in range(4):
                    for k in range(2):
                        h = 2 * part + k
                        for c in range(C2):
                            mm(bank[0][0][:, (c * 8 + h) * 32:(c * 8 + h) * 32 + 32], upw[part][:, k * D + c * 128:k * D + c * 128 + 128],
                               upc[:, 0:32], start=True, stop=True)
                        m = mm(bank[0][1 + h // 4][32 * (h % 4):32 * (h % 4) + 32, 0:D], upc[:, 32:64],
                               upw[part][:, 512 + k * D:512 + k * D + D], start=True, stop=True)
                m.then_inc(prep, 1)
                pe.wait_ge(loaded, 6 * 16)
                for n, (wt, bcol) in enumerate(((yq, "qnb"), (yk, "cnb"), (yv, "cnb"))):
                    for m2 in range(C2):
                        for c in range(C2):
                            m = mm(bank[0][3][:, 2 * n + m2:2 * n + m2 + 1], wt[:, c, m2 * 128:m2 * 128 + 128],
                                   cc(bcol)[:, c:c + 1], start=(c == 0), stop=(c == C2 - 1))
                m.then_inc(prep, 1)

                def batch(s, at):
                    t = Tally(pe)
                    b0, b1, b2, b3 = bank[s]

                    def norm_transposes():
                        t.wait(xn_ready[s])
                        for c in range(C2):
                            m = transpose(b2[:, c * T:(c + 1) * T], XN[s][:, c * 128:(c + 1) * 128], ident[0:T, 0:T])
                        m.then_inc(xt_psum[s], 1)

                    def feature_major(bk, wt, rhs, tiles, sig):
                        n = rhs.shape[2]
                        for j, m2 in enumerate(tiles):
                            for c in range(C2):
                                m = mm(bk[:, j * n:(j + 1) * n], wt[:, c, m2 * 128:(m2 + 1) * 128], rhs[:, c, :],
                                       start=(c == 0), stop=(c == C2 - 1))
                        m.then_inc(sig[s], 1)

                    def token_major(bk, rows, lhs, wt, n0, n1, sig):
                        for c in range(C2):
                            m = mm(bk[0:rows, 0:n1 - n0], lhs[:, c, :], wt[:, c, n0:n1], start=(c == 0), stop=(c == C2 - 1))
                        m.then_inc(sig[s], 1)

                    def output_projection(nt, wt):
                        t.wait(ot_ready[s])
                        for c in range(nt):
                            m = mm(b0[0:T, 0:D], OT[s][:, c, :], wt[:, c, :], start=(c == 0), stop=(c == nt - 1))
                        m.then_inc(y_psum[s], 1)

                    def transpose_o():
                        t.wait(on_ready[s])
                        for c in range(C2):
                            m = transpose(b2[:, c * T:(c + 1) * T], ON[s][:, c * 128:(c + 1) * 128], ident[0:T, 0:T])
                        m.then_inc(ot_psum[s], 1)

                    def context_tile(bk, k):
                        t.wait(cn_ready[s])
                        for c in range(C2):
                            m = transpose(bk[:, c * KP:(c + 1) * KP], CX[s][:, k, c * 128:(c + 1) * 128], ident[0:KP, 0:KP])
                        m.then_inc(ct_psum[s], 1)

                    def transpose_p(u):
                        t.wait(p_ready[s])
                        for h in range(4):
                            m = transpose(b2[0:T, h * T:(h + 1) * T], P[s][0:T, u % 2, h * T:(h + 1) * T], ident[0:T, 0:T])
                        m.then_inc(pt_psum[s], 1)

                    yield 1
                    pe.wait_ge(go[s], at.n[s] + 1)
                    pe.nop().then_inc(started[s], 1)
                    norm_transposes()
                    yield 2
                    t.wait(xt_ready[s])
                    token_major(b0, T, XT[s], qkv0, 0, 384, qkv_psum)
                    yield 3
                    t.wait(c_in[s], 16)
                    for c in range(C2):
                        m = transpose(b1[:, c * T:(c + 1) * T], CX[s][0:T, 0, c * 128:(c + 1) * 128], ident[0:T, 0:T])
                    m.then_inc(ct_psum[s], 1)
                    yield 4
                    t.wait(ct_ready[s])
                    craw = CT[s][:, :, 0:T]
                    feature_major(b3, xk, craw, range(0, 4), kx_psum)
                    yield 5
                    feature_major(b1, xk, craw, range(4, 8), kx_psum)
                    yield 6
                    t.wait(kx_read[s])
                    token_major(b3, T, craw, xv, 0, 512, vx_psum)
                    yield 6
                    t.wait(kx_read[s])
                    token_major(b1, T, craw, xv, 512, 1024, vx_psum)
                    yield 7
                    t.wait(rope_ready[s])
                    for c in range(4):
                        m = transpose(b2[:, c * T:(c + 1) * T], R[s][:, c * 128:(c + 1) * 128], ident[0:T, 0:T])
                    m.then_inc(qk_psum[s], 1)
                    for u in range(6):
                        yield 9 + u
                        if u < 4:
                            t.wait(masked_ready[s])
                            if u == 1:
                                t.wait(vx_read[s], 2)
                            if u >= 2:
                                t.wait(tanh_ready[s])
                            mm(bank[s][u % 2][0:T, 0:QW], KT[s][:, u // 2, 0:T], QM[s][:, u // 2, 4 * (u % 2):4 * (u % 2) + 4, :],
                               start=True, stop=True).then_inc(s_psum[s], 1)
                        if u > 1:
                            v = u - 2
                            t.wait(p_ready[s])
                            for h in range(4):
                                m = mm(b3[0:T, 17 * (4 * v + h):17 * (4 * v + h) + 17], P4[s][v][0:T, h * T:(h + 1) * T],
                                       V0[s][:, v, :], start=True, stop=True)
                            if v == 3:
                                m.then_inc(o_psum[s], 1)
                        if u == 4:
                            t.wait(tanh_ready[s], 2)
                            context_tile(b1, 0)
                    yield 16
                    transpose_o()
                    context_tile(b3, 1)
                    yield 17
                    output_projection(C2, o0)
                    t.wait(ct_ready[s])
                    context_tile(b1, 2)

                    for m2 in range(C2):
                        yield 18 + m2
                        if m2 == 0:
                            t.wait(ct_ready[s], 2)
                        bk = (b3, b1)[m2]
                        for c in range(C2):
                            m = mm(bk[:, 0:LC], yk[:, c, m2 * 128:(m2 + 1) * 128], CT[s][:, c, :], start=(c == 0), stop=(c == 1))
                        m.then_inc(kp_psum[s], 1)
                    yield 19
                    norm_transposes()
                    t.wait(xt_ready[s])
                    feature_major(b2, xq, XT[s], range(0, 4), qx_psum)
                    feature_major(b0, xq, XT[s], range(4, 8), qx_psum)
                    for u in range(6):
                        yield 20 + u
                        if u == 0:
                            t.wait(qx_read[s], 2)
                            t.wait(kp_read[s], 2)
                        if u < 4:
                            bk = bank[s][u % 2]
                            if u >= 2:
                                t.wait(s_shifted[s])
                            mm(bk[0:T, 0:QW], identb, causalb, start=True, stop=True)
                            for k in range(2):
                                m = mm(bk[0:T, k * 2 * T:(k + 1) * 2 * T], QT[s][:, 2 * u + k, :], KM[s][:, 2 * u + k, :, :],
                                       start=False, stop=True, skip_group_check=True)
                            m.then_inc(s_psum[s], 1)
                        if u >= 2:
                            v = u - 2
                            t.wait(pt_ready[s])
                            if v > 0:
                                t.wait(on_ready[s])
                            for h in range(4):
                                m = mm(b3[0:T, 65 * h:65 * h + 65], PT[s][0:T, v % 2, h * T:(h + 1) * T],
                                       V64[s][:, 4 * v + h, :], start=True, stop=True)
                            m.then_inc(o_psum[s], 1)
                        if 1 <= u < 5:
                            transpose_p(u - 1)
                    yield 26
                    t.wait(s_shifted[s], 2)
                    t.wait(on_ready[s])
                    for g in range(2):
                        for c in range(4):
                            m = transpose(bank[s][2 + g][:, c * T:(c + 1) * T], ON[s][:, (4 * g + c) * 128:(4 * g + c + 1) * 128], ident[0:T, 0:T])
                        m.then_inc(ox_psum[s], 1)
                    yield 27
                    t.wait(ot_ready[s])
                    output_projection(FT, xo)

                    yield 29
                    norm_transposes()
                    for k in range(2):
                        m = mm(b3[0:4, k * D:(k + 1) * D], ident[0:T, 8 * k + 1:8 * k + 9:2], XN[s][:, :], start=True, stop=True)
                    m.then_inc(sel_psum[s], 1)
                    yield 30
                    t.wait(xt_ready[s])
                    for c in range(C2):
                        m = mm(b2[0:4, 0:T], XT[s][:, c, 2:10:2], XT[s][:, c, :], start=(c == 0), stop=(c == 1))
                    m.then_inc(g_psum[s], 1)
                    yield 33
                    t.wait(ev_ready[s])
                    t.wait(ew_ready[s])
                    t.wait(g_ready[s])
                    for g in range(2):
                        if g:
                            yield 33
                        for j in range(4):
                            o = bank[s][g][:, j * T:(j + 1) * T]
                            mt = 4 * g + j
                            for c in range(C2):
                                mm(o, f1[:, c, mt * 128:(mt + 1) * 128], XT[s][:, c, :], start=(c == 0), stop=False)
                            m = mm(o, EV[s][:, mt // 2, (mt % 2) * 128:(mt % 2) * 128 + 128], GS[s][:, :], start=False, stop=True)
                        m.then_inc(h_psum[s], 1)
                    yield 33
                    for g in range(2):
                        t.wait(h_ready[s])
                        for j in (2 * g, 2 * g + 1):
                            for c in range(C2):
                                m = mm(b2[0:4, j * T:(j + 1) * T], XT[s][:, c, 10:18:2], QT[s][:, 2 * j + c, :], start=(c == 0), stop=(c == 1))
                    m.then_inc(g_psum[s], 1)
                    yield 36
                    for c in range(FT):
                        mm(b3[0:T, 0:D], QT[s][:, c, :], f2[:, c, :], start=(c == 0), stop=False)
                    t.wait(g_ready[s])
                    for j in range(4):
                        m = mm(b3[0:T, 0:D], G2[s][:, j, :], E2[s][:, j, :], start=False, stop=(j == 3))
                    m.then_inc(y_psum[s], 1)
                    for k in range(2):
                        token_major(bank[s][k], KP, CT[s][:, :, k * KP:(k + 1) * KP], yv, 0, D, vp_psum)

                    yield 39
                    norm_transposes()
                    yield 40
                    t.wait(vp_read[s], 2)
                    t.wait(xt_ready[s])
                    feature_major(b0, k1, XT[s], range(C2), la_psum)
                    feature_major(b1, wqa, XT[s], range(C2), la_psum)
                    token_major(b2, T, XT[s], v1, 0, 64, la_psum)
                    for u in range(4):
                        yield 41 + u
                        if u == 0:
                            t.wait(la_vec[s])
                            t.wait(la_act[s], 2)
                        if u < 2:
                            mm(bank[s][u][0:T, 0:QW], identb, causalb, start=True, stop=False)
                            mm(bank[s][u][0:T, 0:QW], QT[s][:, u, :], KM4[s][:, u, :, :], start=False, stop=True).then_inc(s_psum[s], 1)
                        if u >= 2:
                            v = u - 2
                            t.wait(pt_ready[s])
                            for h in range(4):
                                m = mm(b3[0:T, 33 * (4 * v + h):33 * (4 * v + h) + 33], PT[s][0:T, v, h * T:(h + 1) * T],
                                       V32[s][:, v, :], start=True, stop=True)
                            m.then_inc(pv_done[s] if v < 1 else o_psum[s], 1)
                        if 1 <= u < 3:
                            transpose_p(u - 1)
                    token_major(b1, KP, CT[s][:, :, 2 * KP:3 * KP], yv, 0, D, vp_psum)
                    yield 44
                    transpose_o()
                    yield 45
                    output_projection(C2, woa)

                    yield 47
                    norm_transposes()
                    yield 48
                    t.wait(xt_ready[s])
                    feature_major(b3, yq, XT[s], range(C2), yq_psum)
                    for h in range(H + 2):
                        yield 50 + h
                        if h == 0:
                            t.wait(vp_read[s])
                            t.wait(m_in[s], 16)
                        if h < H:
                            bk = bank[s][h % 2]
                            if h % 4 == 0:
                                t.wait(masked_ready[s])
                            mm(bk[0:T, 0:LC], onesb, MR[s][:, :], start=True, stop=False)
                            mm(bk[0:T, 0:LC], QM[s][:, h // 8, h % 8, :], KT[s][:, h // 8, :], start=False, stop=True).then_inc(s_psum[s], 1)
                        if h >= 2:
                            v = h - 2
                            t.wait(pt_ready[s])
                            for k in range(KT3):
                                m = mm(b3[0:T, 17 * v:17 * v + 17], PT[s][0:KP, v % 2, k * T:(k + 1) * T],
                                       V16[s][:, k, v, :], start=(k == 0), stop=(k == KT3 - 1))
                            m.then_inc(pv_done[s] if v < H - 1 else o_psum[s], 1)
                        if 1 <= h < H + 1:
                            v = h - 1
                            t.wait(p_ready[s])
                            for k in range(KT3):
                                m = transpose(b2[0:KP, k * T:(k + 1) * T], P[s][0:T, v % 2, k * KP:(k + 1) * KP], ident[0:T, 0:T])
                            m.then_inc(pt_psum[s], 1)
                    yield 68
                    transpose_o()
                    yield 68
                    output_projection(C2, yo)

                    yield 71
                    t.wait(xn_ready[s])
                    for c in range(C2):
                        m = mm(b2[:, c:c + 1], XN[s][:, c * 128:(c + 1) * 128], const[0:T, KC["ones"][0]:KC["ones"][1]], start=True, stop=True)
                    m.then_inc(mean_psum[s], 1)
                    yield 71
                    t.wait(mean_ready[s])
                    for c in range(C2):
                        m = mm(b3[0:1, 0:E], xbar[s][:, c:c + 1], gate[:, c, :], start=(c == 0), stop=(c == 1))
                    m.then_inc(logit_psum[s], 1)
                run_slots(pe, half, batch, BEATS_A)
                for s in SLOTS:
                    pe.wait_ge(go[s], half + 1)

            @block.scalar
            def _(act):
                A = nc.scalar.activation

                def batch(s, at):
                    t = Tally(act)
                    b0, b1, b2, b3 = bank[s]

                    def copy2(dst, bk, n, ready, done, scale=1.0):
                        t.wait(ready[s])
                        A(dst, bk[:, 0:C2 * n].rearrange("p (c q) -> p c q", c=C2), ACT.Copy, scale=scale).then_inc(done[s], 1)

                    def copy_xt():
                        copy2(XT[s][:, :, :], b2, T, xt_psum, xt_ready)

                    def copy_pt(u, free):
                        t.wait(pt_psum[s])
                        if u >= 2:
                            t.wait(free[s])
                        A(PT[s][0:T, u % 2, :], b2[0:T, 0:QW], ACT.Copy).then_inc(pt_ready[s], 1)

                    def copy_context(bk, k):
                        copy2(CT[s][:, :, k * KP:(k + 1) * KP], bk, KP, ct_psum, ct_ready)

                    yield 2
                    act.wait_ge(go[s], at.n[s] + 1)
                    act.nop().then_inc(started[s], 1)
                    copy_xt()
                    yield 3
                    t.wait(qkv_psum[s])
                    A(SQ[s][:, :], b0[0:T, 0:320], ACT.Square)
                    A(V0[s][:, :, 0:16], b0[0:T, 320:384].rearrange("p (g d) -> p g d", g=4), ACT.Copy).then_inc(sq_ready[s], 1)
                    copy2(CT[s][:, :, 0:T], b1, T, ct_psum, ct_ready)
                    for k in range(2):
                        yield 6 + k
                        t.wait(vx_psum[s])
                        A(V64[s][:, 8 * k:8 * k + 8, 0:64], (b3, b1)[k][0:T, 0:512].rearrange("p (h d) -> p h d", h=8), ACT.Copy).then_inc(vx_read[s], 1)
                    t.wait(qk_psum[s])
                    A(KT[s][:, :, 0:T], b2[:, C2 * T:2 * C2 * T].rearrange("p (c q) -> p c q", c=C2), ACT.Copy).then_inc(qk_copied[s], 1)
                    for u in range(4):
                        yield 9 + u
                        t.wait(s_psum[s])
                        A(P4[s][u], bank[s][u % 2][0:T, 0:QW], ACT.Tanh, scale=1.0 / (4.0 * CAP)).then_inc(tanh_ready[s], 1)
                        t.wait(tanh_ready[s])
                        A(P4[s][u], P4[s][u], ACT.Exp, scale=CAP).then_inc(exp_ready[s], 1)
                    yield 13
                    copy_context(b1, 0)
                    yield 16
                    copy2(OT[s][:, 0:C2, :], b2, T, ot_psum, ot_ready)
                    copy_context(b3, 1)
                    yield 17
                    copy_context(b1, 2)
                    for m2 in range(C2):
                        yield 18 + m2
                        t.wait(kp_psum[s])
                        A(KT[s][:, m2, :], (b3, b1)[m2][:, 0:LC], ACT.Identity, bias=bfold[:, 2 + m2:3 + m2]).then_inc(kp_read[s], 1)

                    yield 19
                    copy_xt()
                    t.skip(o_psum[s], 1)
                    for u in range(5):
                        yield 20 + u
                        if u < 4:
                            t.wait(s_shifted[s])
                            A(P[s][0:T, u % 2, :], P[s][0:T, u % 2, :], ACT.Exp).then_inc(p_ready[s], 1)
                        if u > 0:
                            copy_pt(u - 1, o_psum)
                    t.skip(o_psum[s], 2)

                    yield 30
                    copy_xt()
                    t.wait(sel_psum[s])
                    A(ev[s], b3[0:4, 0:2 * D], ACT.Copy).then_inc(ev_ready[s], 1)
                    t.wait(g_psum[s])
                    A(GS[s][:, :], b2[0:4, 0:T], ACT.Copy, scale=cc("scale")[0:4, :]).then_inc(g_ready[s], 1)
                    for g in range(2):
                        yield 32 + g
                        t.wait(h_psum[s])
                        for j in range(4):
                            mt = 4 * g + j
                            m = A(QT[s][:, mt, :], bank[s][g][:, j * T:(j + 1) * T], ACT.Gelu, bias=cc("fb1")[:, mt:mt + 1])
                        m.then_inc(h_ready[s], 1)
                    yield 36
                    t.wait(g_psum[s])
                    A(G2[s][:, :, :], b2[0:4, 0:QW].rearrange("p (j q) -> p j q", j=4), ACT.Copy, scale=cc("scale")[0:4, :]).then_inc(g_ready[s], 1)
                    yield 37
                    for k in range(2):
                        t.wait(vp_psum[s])
                        A(V16[s][:, k, :, 0:16], bank[s][k][0:KP, 0:D].rearrange("p (h d) -> p h d", h=H), ACT.Copy).then_inc(vp_read[s], 1)

                    yield 40
                    copy_xt()
                    yield 41
                    t.wait(la_psum[s])
                    copy2(QT[s][:, 0:C2, :], b1, T, la_psum, la_act, scale=128 ** -0.5)
                    t.wait(la_psum[s])
                    A(V32[s][:, :, 0:32], b2[0:T, 0:64].rearrange("p (g d) -> p g d", g=2), ACT.Copy).then_inc(la_act[s], 1)
                    for u in range(3):
                        yield 41 + u
                        if u < 2:
                            t.wait(s_shifted[s])
                            A(P[s][0:T, u % 2, :], P[s][0:T, u % 2, :], ACT.Exp).then_inc(p_ready[s], 1)
                        if u > 0:
                            copy_pt(u - 1, None)
                    yield 44
                    t.wait(vp_psum[s])
                    A(V16[s][:, 2, :, 0:16], b1[0:KP, 0:D].rearrange("p (h d) -> p h d", h=H), ACT.Copy).then_inc(vp_read[s], 1)
                    copy2(OT[s][:, 0:C2, :], b2, T, ot_psum, ot_ready)

                    yield 47
                    copy_xt()
                    yield 47
                    t.skip(pv_done[s], 1)
                    for h in range(H + 1):
                        yield 50 + h
                        if h < H:
                            t.wait(s_shifted[s])
                            A(P[s][0:T, h % 2, 0:LC], bank[s][h % 2][0:T, 0:LC], ACT.Exp, bias=mx[s][:, h:h + 1]).then_inc(p_ready[s], 1)
                        if h > 0:
                            v = h - 1
                            t.wait(pt_psum[s])
                            if v >= 2:
                                t.wait(pv_done[s])
                            A(PT[s][0:KP, v % 2, 0:KT3 * T], b2[0:KP, 0:KT3 * T], ACT.Copy).then_inc(pt_ready[s], 1)
                    yield 68
                    t.wait(ot_psum[s])
                    A(OT[s][:, 0, :], b2[:, 0:T], ACT.Identity, bias=bfold[:, 4:5])
                    A(OT[s][:, 1, :], b2[:, T:2 * T], ACT.Identity, bias=bfold[:, 5:6]).then_inc(ot_ready[s], 1)
                    yield 72
                    t.wait(mean_psum[s])
                    A(xbar[s][:, :], b2[:, 0:C2], ACT.Copy, scale=1.0 / T).then_inc(mean_ready[s], 1)
                    yield 72
                    t.wait(logit_psum[s])
                    A(lrow[s][:, :], b3[0:1, 0:E], ACT.Copy).then_inc(logit_ready[s], 1)
                run_slots(act, half, batch, BEATS_A)
                for s in SLOTS:
                    act.wait_ge(go[s], half + 1)

            @block.vector
            def _(dve):
                v = nc.vector
                t = Tally(dve)
                chain = prep_vec
                dve.wait_ge(loaded, 6 * 16)
                v.tensor_copy(constb[:, :], kbw)
                v.tensor_copy(mfl[:, :], mwords[:, :]).then_inc(chain, 1)
                t.wait(chain)
                v.tensor_reduce(mall[:, :], mfl[:, :], AX_X, ALU.min).then_inc(chain, 1)
                t.wait(chain)
                v.tensor_tensor(mfl[:, 0:1], mfl[:, 0:1], mall[:, :], ALU.subtract).then_inc(chain, 1)
                t.wait(chain)
                v.tensor_scalar(mneg[:, :], mfl[:, :], NEG, None, ALU.mult).then_inc(mask_ready, 1)
                v.tensor_scalar(bq8[:, :], cc("xbq"), 0.125, None, ALU.mult)
                for s in SLOTS:
                    v.memset(V0[s][:, :, 16:17], 1.0)
                    v.memset(V64[s][:, :, 64:65], 1.0)
                    v.memset(V32[s][:, :, 32:33], 1.0)
                    v.memset(V16[s][:, :, :, 16:17], 1.0)
                    v.memset(KM4[s][:, :, :, :], 0.0)
                dve.wait_ge(prep, 2)
                for s in SLOTS:
                    v.memset(KM[s][:, :, :, :], 0.0)
                for c in range(C2):
                    v.tensor_copy(wqa[:, c, :], bank[0][0][:, c * D:(c + 1) * D])
                    v.tensor_copy(woa[:, c, :], bank[0][1 + c][:, 0:D])
                a = CA["ybq"][0]
                v.tensor_tensor(bfold[:, 0:6], bank[0][3][:, 0:6], col[:, a:a + 6], ALU.add).then_inc(chain, 1)
                t.wait(chain)
                v.tensor_scalar(bfold[:, 8:10], bfold[:, 0:2], 0.25, None, ALU.mult)
                for wt, name, scale in ((yq, "qnw", 0.25), (yk, "cnw", 1.0), (yv, "cnw", 1.0)):
                    for c in range(C2):
                        v.tensor_scalar(wt[:, c, :], wt[:, c, :], cc(name)[:, c:c + 1], scale, ALU.mult, ALU.mult)
                dve.drain().then_inc(all_prepared, 1)

                def batch(s, at):
                    t = Tally(dve)
                    b0, b1, b2, b3 = bank[s]

                    def chained(ins):
                        ins.then_inc(vec_done[s], 1)
                        t.wait(vec_done[s])

                    def layernorm(src):
                        chained(v.bn_stats(st6[s][0:T, 0, :], src[s][:, :]))
                        chained(v.bn_aggr(mv[s][0:T, 0, :], st6[s][0:T, 0, :]))
                        v.tensor_scalar(var[s][0:T, 0:1], mv[s][0:T, 0, 1:2], EPS, None, ALU.add).then_inc(ln_var[s], 1)

                    def normalise(src, bias=None):
                        t.wait(ln_rstd[s])
                        v.tensor_scalar(XN[s][:, :], src[s][:, :], mv[s][0:T, 0, 0:1], rstd[s][0:T, 0:1], ALU.subtract, ALU.mult).then_inc(xn_ready[s], 1)
                        if bias is not None:
                            chained(v.tensor_tensor(src[s][:, :], src[s][:, :], bias, ALU.add))

                    def shift(u):
                        t.wait(s_psum[s])
                        sc = bank[s][u % 2][0:T, 0:QW].rearrange("p (h k) -> p h k", h=4)
                        if u >= 2:
                            t.wait(pt_psum[s])
                        top = mx[s][:, 4 * (u % 2):4 * (u % 2) + 4]
                        chained(v.tensor_reduce(top, sc, AX_X, ALU.max))
                        v.tensor_tensor(P[s][0:T, u % 2, :].rearrange("p (h k) -> p h k", h=4), sc,
                                        top.unsqueeze(2).to_broadcast((T, 4, T)), ALU.subtract).then_inc(s_shifted[s], 1)

                    def mask_queries(u, bk, bias):
                        c, half_ = u // 2, slice(4 * (u % 2), 4 * (u % 2) + 4)
                        q = bk[:, c * T:(c + 1) * T].unsqueeze(1).to_broadcast((128, 4, T))
                        if bias is None:
                            v.tensor_tensor(QM[s][:, c, half_, :], q, hm8[:, half_, :], ALU.mult).then_inc(masked_ready[s], 1)
                        else:
                            v.scalar_tensor_tensor(out=QM[s][:, c, half_, :], in0=q, scalar=bias[:, c:c + 1], in1=hm8[:, half_, :],
                                                   op0=ALU.add, op1=ALU.mult).then_inc(masked_ready[s], 1)

                    def causal(u):
                        t.wait(exp_ready[s])
                        p3 = P4[s][u].rearrange("p (h k) -> p h k", h=4)
                        v.tensor_tensor(p3, p3, tri.unsqueeze(1).to_broadcast((T, 4, T)), ALU.mult).then_inc(p_ready[s], 1)

                    def normalise_o(nh, hd, at_col=0):
                        t.wait(o_psum[s])
                        o = b3[0:T, 0:nh * (hd + 1)].rearrange("p (h d) -> p h d", h=nh)
                        chained(v.reciprocal(rec[s][:, 0:nh], o[:, :, hd]))
                        v.tensor_tensor(ON[s][:, at_col:at_col + nh * hd].rearrange("p (h d) -> p h d", h=nh), o[:, :, 0:hd],
                                        rec[s][:, 0:nh].unsqueeze(2).to_broadcast((T, nh, hd)), ALU.mult).then_inc(on_ready[s], 1)

                    def residual(bk, src=X):
                        t.wait(y_psum[s])
                        chained(v.tensor_tensor(X[s][:, :], src[s][:, :], bk[0:T, 0:D], ALU.add))

                    yield 0
                    dve.wait_ge(go[s], at.n[s] + 1)
                    dve.nop().then_inc(started[s], 1)
                    layernorm(XIN)
                    yield 0
                    normalise(XIN)
                    yield 3
                    t.wait(sq_ready[s])
                    chained(v.tensor_reduce(var[s][0:T, 0:20], SQ[s][:, :].rearrange("p (h d) -> p h d", h=20), AX_X, ALU.add))
                    v.tensor_scalar(var[s][0:T, 0:20], var[s][0:T, 0:20], 1.0 / 16, EPS, ALU.mult, ALU.add).then_inc(rms_var[s], 1)

                    def cross_keys(g):
                        t.wait(kx_psum[s])
                        for hh in range(2):
                            r = slice(64 * hh, 64 * hh + 64)
                            m = v.tensor_tensor(KM[s][r, 4 * g:4 * g + 4, hh, :], (b3, b1)[g][r, 0:QW].rearrange("p (c q) -> p c q", c=4),
                                                cc("xbk")[r, 4 * g:4 * g + 4].unsqueeze(2).to_broadcast((64, 4, T)), ALU.add)
                        m.then_inc(kx_read[s], 1)
                    yield 5
                    cross_keys(0)
                    yield 6
                    cross_keys(1)
                    t.wait(rms_rstd[s])
                    q3 = QKN[s][:, :].rearrange("p (h d) -> p h d", h=20)
                    chained(v.tensor_tensor(q3, b0[0:T, 0:320].rearrange("p (h d) -> p h d", h=20),
                                            rstd[s][0:T, 0:20].unsqueeze(2).to_broadcast((T, 20, 16)), ALU.mult))
                    t3 = T2[s][:, :].rearrange("p (h d) -> p h d", h=20)
                    v.tensor_tensor(t3[:, :, 0:8], q3[:, :, 8:16], sin[:, 0:8].unsqueeze(1).to_broadcast((T, 20, 8)), ALU.mult)
                    chained(v.tensor_tensor(t3[:, :, 8:16], q3[:, :, 0:8], sin[:, 8:16].unsqueeze(1).to_broadcast((T, 20, 8)), ALU.mult))
                    chained(v.tensor_tensor(q3, q3, cos.unsqueeze(1).to_broadcast((T, 20, 16)), ALU.mult))
                    v.tensor_tensor(R[s][:, 0:D], QKN[s][:, 0:D], T2[s][:, 0:D], ALU.add)
                    v.tensor_tensor(R[s][:, D:2 * D].rearrange("p (g r d) -> p g r d", g=4, r=4),
                                    q3[:, 16:20, :].unsqueeze(2).to_broadcast((T, 4, 4, 16)),
                                    t3[:, 16:20, :].unsqueeze(2).to_broadcast((T, 4, 4, 16)), ALU.add).then_inc(rope_ready[s], 1)
                    yield 7
                    t.wait(qk_psum[s])
                    t.wait(qk_copied[s])
                    for u in range(4):
                        if u == 2:
                            yield 8
                        mask_queries(u, b2, None)
                    yield 9
                    for k in range(KT3):
                        v.bn_stats(cst6[s][:, k, :], CX[s][:, k, :]).then_inc(vec_done[s], 1)
                    t.wait(vec_done[s], KT3)
                    for k in range(KT3):
                        v.bn_aggr(cmv[s][:, k, :], cst6[s][:, k, :]).then_inc(vec_done[s], 1)
                    t.wait(vec_done[s], KT3)
                    v.tensor_scalar(cvar[s][:, :], cmv[s][:, :, 1], EPS, None, ALU.add).then_inc(cn_var[s], 1)
                    for u in range(2):
                        yield 9 + u
                        causal(u)
                    t.wait(cn_rstd[s])
                    for k in range(KT3):
                        v.tensor_scalar(CX[s][:, k, :], CX[s][:, k, :], cmv[s][:, k, 0:1], crstd[s][:, k:k + 1],
                                        ALU.subtract, ALU.mult).then_inc(cn_ready[s], 1)
                    for u in range(2, 4):
                        yield 9 + u
                        causal(u)
                    yield 15
                    normalise_o(H, 16)
                    yield 17
                    residual(b0, XIN)
                    layernorm(X)

                    yield 18
                    normalise(X, rr("xbo"))
                    yield 19
                    for g in range(2):
                        t.wait(qx_psum[s])
                        v.scalar_tensor_tensor(out=QT[s][:, 4 * g:4 * g + 4, :], in0=(b2, b0)[g][:, 0:QW].rearrange("p (c q) -> p c q", c=4),
                                               scalar=0.125, in1=bq8[:, 4 * g:4 * g + 4].unsqueeze(2).to_broadcast((128, 4, T)),
                                               op0=ALU.mult, op1=ALU.add).then_inc(qx_read[s], 1)
                    t.skip(s_psum[s], 4)
                    for u in range(6):
                        yield 20 + u
                        if u < 4:
                            shift(u)
                        if u >= 2:
                            normalise_o(4, 64, (u - 2) * D)
                    t.skip(pt_psum[s], 2)
                    yield 26
                    for g in range(2):
                        t.wait(ox_psum[s])
                        v.tensor_tensor(OT[s][:, 4 * g:4 * g + 4, :], bank[s][2 + g][:, 0:QW].rearrange("p (c q) -> p c q", c=4),
                                        cc("xbv")[:, 4 * g:4 * g + 4].unsqueeze(2).to_broadcast((128, 4, T)), ALU.add).then_inc(ot_ready[s], 1)
                    yield 28
                    residual(b0)
                    layernorm(X)

                    yield 29
                    normalise(X, rr("fb2"))
                    yield 30
                    t.wait(ev_ready[s])
                    for k in range(4):
                        v.tensor_scalar(E2[s][:, :, 64 * k:64 * k + 64], ev[s][:, D:2 * D].rearrange("p (r j) -> p j r", j=4),
                                        ident[0:4, k:k + 1], None, ALU.mult)
                        m = v.tensor_scalar(EV[s][:, k, :], ev[s][:, 0:D], ident[0:4, k:k + 1], None, ALU.mult)
                    m.then_inc(ew_ready[s], 1)
                    yield 37
                    residual(b3)
                    layernorm(X)

                    yield 38
                    normalise(X)
                    yield 40
                    t.wait(la_psum[s])
                    for hh in range(4):
                        r = slice(32 * hh, 32 * hh + 32)
                        m = v.tensor_copy(KM4[s][r, :, hh, :], b0[r, 0:C2 * T].rearrange("p (c q) -> p c q", c=C2))
                    m.then_inc(la_vec[s], 1)
                    for u in range(2):
                        yield 41 + u
                        shift(u)
                    yield 44
                    normalise_o(8, 32)
                    yield 45
                    residual(b0)
                    layernorm(X)

                    yield 46
                    normalise(X, rr("ybo"))
                    yield 48
                    t.wait(yq_psum[s])
                    for u in range(4):
                        mask_queries(u, b3, bfold[:, 8:10])
                    for h in range(H):
                        yield 50 + h
                        t.wait(s_psum[s])
                        v.tensor_reduce(mx[s][:, h:h + 1], bank[s][h % 2][0:T, 0:LC], AX_X, ALU.max, negate=True).then_inc(s_shifted[s], 1)
                    yield 67
                    normalise_o(H, 16)
                    yield 70
                    residual(b0)
                    layernorm(X)
                    yield 71
                    normalise(X)
                run_slots(dve, half, batch, BEATS_A)
                for s in SLOTS:
                    dve.wait_ge(go[s], half + 1)

            @block.gpsimd
            def _(pool):
                g = nc.gpsimd
                nhalf = sa("nhalf", [128, 20])
                g.memset(nhalf[:, :], -0.5).then_inc(halves_ready, 1)
                pool.wait_ge(halves_ready, 1)

                def batch(s, at):
                    t = Tally(pool)

                    def inverse_root():
                        t.wait(ln_var[s])
                        g.tensor_tensor(rstd[s][0:T, 0:1], var[s][0:T, 0:1], nhalf[0:T, 0:1], ALU.pow).then_inc(ln_rstd[s], 1)

                    yield 0
                    pool.wait_ge(go[s], at.n[s] + 1)
                    pool.nop().then_inc(started[s], 1)
                    inverse_root()
                    yield 3
                    t.wait(rms_var[s])
                    g.tensor_tensor(rstd[s][0:T, :], var[s][0:T, :], nhalf[0:T, :], ALU.pow).then_inc(rms_rstd[s], 1)
                    yield 9
                    t.wait(cn_var[s])
                    g.tensor_tensor(crstd[s][:, :], cvar[s][:, :], nhalf[0:KP, 0:KT3], ALU.pow).then_inc(cn_rstd[s], 1)
                    yield 17
                    inverse_root()
                    yield 28
                    inverse_root()
                    yield 37
                    inverse_root()
                    yield 45
                    inverse_root()
                    yield 70
                    inverse_root()
                run_slots(pool, half, batch, BEATS_A)
                for s in SLOTS:
                    pool.wait_ge(go[s], half + 1)


        routed = sem("routed")
        route_vec = sem("route_vec")
        route_pe = sem("route_pe")
        route_act = sem("route_act")
        route_dma = sem("route_dma")
        added = sem("added")
        go_last = pair("go_last")
        gate_shifted, gate_exp = sem("gate_shifted"), sem("gate_exp")
        NI = B * TOPK
        base = half + 1
        with ExitStack() as phase:
            def sa(name, shape, dt=F32):
                return phase.enter_context(nc.sbuf_tensor(name, shape, dt))

            def two(name, shape, dt=F32):
                return [sa(f"{name}{s}", shape, dt) for s in SLOTS]

            wexp, rexp = two("wexp", [128, NWE]), two("rexp", [T, NRE])
            gates = sa("gates", [T, NI])
            items = sa("items", [1, 2 * NI + 2], I32)
            rt = sa("rt", [B, NRT])
            lgt, gbt = sa("lgt", [B, E]), sa("gbt", [B, E])
            cmp1, cmp2 = sa("cmp1", [B, E, E]), sa("cmp2", [B, E, E])
            rank, member, gmax, gexp, gsum, gw = (sa("rank", [B, E]), sa("member", [B, E]), sa("gmax", [B, 1]),
                                                  sa("gexp", [B, E]), sa("gsum", [B, 1]), sa("gw", [B, E]))
            tot, pos = sa("tot", [B, E]), sa("pos", [B, E])
            vals = sa("vals", [B, E, 3])
            onehot = sa("onehot", [B, E, NI])
            listf, listi = sa("listf", [3, NI]), sa("listi", [2, NI], I32)
            iota = rt[:, 0:NI]
            below = rt[:, NI:NI + B]
            lower = rt[:, NI + B:NI + B + E * E].rearrange("p (a c) -> p a c", a=E)
            bidx = rt[:, NI + B + E * E:NI + B + E * E + 1 + E]
            onesq = sa("onesq", [B, B])

            XIN = two("BXIN", [T, D])
            X, Z, Y = two("BX", [T, D]), two("BZ", [T, D]), two("BY", [T, D])
            ZN = two("ZN", [T, D])
            XT, ZT, QT, KT = (two("BXT", [128, C2, T]), two("BZT", [128, C2, T]), two("BQT", [128, C2, T]),
                              two("BKT", [128, C2, T]))
            KM = two("BKM", [128, C2, 8, T])
            V16 = two("BV16", [T, H, 17])
            P, PT = two("BP", [T, 2, QW]), two("BPT", [T, 2, QW])
            mx, rec = two("Bmx", [T, 8]), two("Brec", [T, H])
            ON, OT, HT = two("BON", [T, D]), two("BOT", [128, C2, T]), two("BHT", [128, FT, T])
            st6, mv, var, rstd = two("Bst6", [T, 6]), two("Bmv", [T, 2]), two("Bvar", [T, 1]), two("Brstd", [T, 1])
            nhalf = sa("Bnhalf", [T, 1])

            hidden_banks = [[bank[s][k] for k in (0, 1, 2, 0)] for s in SLOTS]

            def W(s, name, c):
                a, b = WE[name]
                return wexp[s][:, a:b].rearrange("p (c n) -> p c n", c=c)

            def wc(s, name):
                a, b = WE[name]
                return wexp[s][:, a:b]

            def rr(s, name):
                a, b = RE[name]
                return rexp[s][:, a:b]

            block = phase.enter_context(nc.Block())

            @block.sync
            def _(sp):
                sp.dma_start(lgt[:, :], lg).then_inc(route_dma, 16)
                sp.dma_start(gbt[:, :], gb.to_broadcast((B, E))).then_inc(route_dma, 16)
                sp.wait_ge(routed, 1)
                sp.dma_start(sel[0:1, :], listf[2:3, :]).then_inc(route_dma, 16)
                sp.dma_start(items[0:1, 0:NI], listi[0:1, :]).then_inc(route_dma, 16)
                sp.dma_start(items[0:1, NI + 1:NI + 1 + B], listi[1:2, 0:B]).then_inc(route_dma, 16)
                sp.dma_start(items[0:1, NI + 2 + B:2 * NI + 2], listi[1:2, B:NI]).then_inc(route_dma, 16)
                sp.wait_ge(route_dma, 16 * 6)
                sp.dma_start(gates[:, :], sel[0:1, :].to_broadcast((T, NI))).then_inc(route_dma, 16)

                def load_x(s, n):
                    b = sp.value_load(items[0:1, bass.ds(n + s * B, 1)], min_val=0, max_val=B - 1)
                    sp.dma_start(XIN[s][:, :], xmid[bass.ds(b, 1), :, :].rearrange("a t d -> (a t) d")).then_inc(x_in[s], 16)

                def change(s, n):
                    old = sp.value_load(items[0:1, bass.ds(n + (NI + s * (B + 1)), 1)], min_val=-1, max_val=E - 1)
                    new = sp.value_load(items[0:1, bass.ds(n + (NI + s * (B + 1) + 1), 1)], min_val=0, max_val=E - 1)
                    return old, new

                def load_weights(s, n):
                    old, new = change(s, n)
                    with sp.If(old != new):
                        late = WE["o"][0]
                        sp.dma_start(wexp[s][:, 0:late], we[bass.ds(new, 1), :, 0:late].rearrange("a p n -> (a p) n")).then_inc(c_in[s], 16)
                        sp.dma_start(wexp[s][:, late:NWE], we[bass.ds(new, 1), :, late:NWE].rearrange("a p n -> (a p) n")).then_inc(late_in[s], 16)
                    with sp.Else():
                        sp.sem_inc(c_in[s], 16)
                        sp.sem_inc(late_in[s], 16)
                    sp.nop()

                def load_rows(s, n):
                    old, new = change(s, n)
                    with sp.If(old != new):
                        sp.dma_start(rexp[s][:, :], re_[bass.ds(new, 1), :].to_broadcast((T, NRE))).then_inc(m_in[s], 16)
                    with sp.Else():
                        sp.sem_inc(m_in[s], 16)
                    sp.nop()
                for s in SLOTS:
                    load_x(s, 0)
                sp.wait_ge(route_dma, 16 * 7)
                for s in SLOTS:
                    sp.wait_ge(x_in[s], 16)
                    sp.sem_clear(slot_sems[s]).then_inc(go_last[s], 1)
                    load_weights(s, 0)
                    load_rows(s, 0)
                sp.sem_inc(routed, 1)

                def batch(s, at):
                    t = Tally(sp)
                    yield 0
                    yield 19
                    if not at.last:
                        t.wait(xt_psum[s])
                        t.wait(m_taken[s])
                        load_x(s, at.n[s] + 1)
                    yield 24
                    t.wait(ln_var[s], 2)
                    if not at.last:
                        t.wait(x_in[s], 16)
                    sp.sem_clear(first_sems[s]).then_inc(go[s], 1)
                    if not at.last:
                        load_weights(s, at.n[s] + 1)
                    yield 25
                    t.wait(y_taken[s])
                    sp.sem_clear(last_sems[s]).then_inc(go_last[s], 1)
                    if not at.last:
                        load_rows(s, at.n[s] + 1)
                run_slots(sp, B, batch, BEATS_B)
                sp.wait_ge(added, 16 + 32 * B)

            @block.tensor
            def _(pe):
                mm, transpose = nc.tensor.matmul, nc.tensor.transpose
                pe.wait_ge(added, 16)
                pe.wait_ge(route_act, 1)
                mm(bank[0][0][0:B, 0:E], below, member[:, :], start=True, stop=True)
                mm(bank[0][1][0:B, 0:E], onesq[:, :], member[:, :], start=True, stop=True).then_inc(route_pe, 1)
                pe.wait_ge(route_act, 2)
                for e in range(E):
                    m = mm(bank[0][2][0:3, 0:NI], vals[:, e, :], onehot[:, e, :], start=(e == 0), stop=(e == E - 1))
                m.then_inc(route_pe, 1)
                pe.wait_ge(routed, 2)

                def batch(s, at):
                    t = Tally(pe)
                    b0, b1, b2, b3 = bank[s]

                    def transposes(src, done):
                        for c in range(C2):
                            m = transpose(b2[:, c * T:(c + 1) * T], src[s][:, c * 128:(c + 1) * 128], ident[0:T, 0:T])
                        m.then_inc(done[s], 1)

                    def feature_major(bk, wt, n0, tiles, rhs, sig):
                        for j in range(tiles):
                            for c in range(C2):
                                m = mm(bk[:, j * T:(j + 1) * T], wt[:, c, n0 + j * 128:n0 + (j + 1) * 128], rhs[:, c, :],
                                       start=(c == 0), stop=(c == 1))
                        m.then_inc(sig[s], 1)

                    yield 0
                    pe.wait_ge(go[s], at.n[s] + base)
                    pe.nop().then_inc(started[s], 1)
                    transposes(XIN, xt_psum)
                    yield 1
                    t.wait(xt_ready[s])
                    t.wait(c_in[s], 16)
                    qkv = W(s, "qkv", C2)
                    feature_major(b2, qkv, D, C2, XT[s], qkv_psum)
                    yield 2
                    feature_major(b0, qkv, 0, C2, XT[s], qkv_psum)
                    yield 3
                    for c in range(C2):
                        m = mm(b3[0:T, 0:D], XT[s][:, c, :], qkv[:, c, 2 * D:3 * D], start=(c == 0), stop=(c == 1))
                    m.then_inc(qkv_psum[s], 1)

                    def scores(u):
                        if u < 2:
                            t.wait(masked_ready[s])
                        if u >= 2:
                            t.wait(s_shifted[s])
                        mm(bank[s][u % 2][0:T, 0:QW], QT[s][:, u // 2, :], KM[s][:, u // 2, 4 * (u % 2):4 * (u % 2) + 4, :],
                           start=True, stop=True).then_inc(s_psum[s], 1)

                    def transpose_p(u):
                        t.wait(p_ready[s])
                        for h in range(4):
                            m = transpose(b2[0:T, h * T:(h + 1) * T], P[s][:, u % 2, h * T:(h + 1) * T], ident[0:T, 0:T])
                        m.then_inc(pt_psum[s], 1)

                    def weigh_values(u):
                        t.wait(pt_ready[s])
                        for h in range(4):
                            m = mm(b3[0:T, 17 * (4 * u + h):17 * (4 * u + h) + 17], PT[s][:, u % 2, h * T:(h + 1) * T],
                                   V16[s][:, 4 * u + h, :], start=True, stop=True)
                        m.then_inc(pv_done[s] if u < 3 else o_psum[s], 1)
                    yield 4
                    t.wait(qx_read[s])
                    scores(0)
                    yield 4
                    t.wait(vx_read[s])
                    scores(1)
                    yield 6
                    t.wait(masked_ready[s], 2)
                    transpose_p(0)
                    yield 6
                    scores(2)
                    yield 8
                    weigh_values(0)
                    transpose_p(1)
                    yield 9
                    scores(3)
                    yield 10
                    weigh_values(1)
                    transpose_p(2)
                    yield 12
                    weigh_values(2)
                    transpose_p(3)
                    yield 14
                    weigh_values(3)
                    yield 15
                    t.wait(on_ready[s])
                    transposes(ON, ot_psum)
                    yield 16
                    t.wait(late_in[s], 16)
                    t.wait(ot_ready[s])
                    for c in range(C2):
                        m = mm(b0[0:T, 0:D], OT[s][:, c, :], W(s, "o", C2)[:, c, :], start=(c == 0), stop=(c == 1))
                    m.then_inc(y_psum[s], 1)
                    yield 18
                    t.wait(xn_ready[s])
                    transposes(ZN, xt_psum)
                    l1 = W(s, "l1", C2)
                    for g in range(FT // 2 + 2):
                        yield 18 + g
                        if g == 0:
                            t.wait(xt_ready[s])
                        if g < FT // 2:
                            feature_major(hidden_banks[s][g], l1, 256 * g, 2, ZT[s], h_psum)
                        if g >= 2:
                            t.wait(h_ready[s])
                            for mt in (2 * g - 4, 2 * g - 3):
                                m = mm(b3[0:T, 0:D], HT[s][:, mt, :], W(s, "l2", FT)[:, mt, :], start=(mt == 0), stop=(mt == FT - 1))
                    m.then_inc(y_psum[s], 1)
                run_slots(pe, B, batch, BEATS_B)

            @block.scalar
            def _(act):
                A = nc.scalar.activation
                act.wait_ge(gate_shifted, 1)
                A(gexp[:, :], gw[:, :], ACT.Exp, accum_out=gsum[:, :]).then_inc(gate_exp, 1)
                act.wait_ge(routed, 2)

                def batch(s, at):
                    t = Tally(act)
                    b0, b1, b2, b3 = bank[s]

                    def copy2(dst, ready, done):
                        t.wait(ready[s])
                        A(dst[s][:, :, :], b2[:, 0:C2 * T].rearrange("p (c q) -> p c q", c=C2), ACT.Copy).then_inc(done[s], 1)

                    yield 1
                    act.wait_ge(go[s], at.n[s] + base)
                    act.nop().then_inc(started[s], 1)
                    copy2(XT, xt_psum, xt_ready)
                    yield 2
                    t.wait(qkv_psum[s], 2)
                    for m2 in range(C2):
                        m = A(QT[s][:, m2, :], b0[:, m2 * T:(m2 + 1) * T], ACT.Identity, bias=wc(s, "bq")[:, m2:m2 + 1])
                    m.then_inc(qx_read[s], 1)
                    yield 3
                    t.wait(qkv_psum[s])
                    A(V16[s][:, :, 0:16], b3[0:T, 0:D].rearrange("p (h d) -> p h d", h=H), ACT.Copy).then_inc(vx_read[s], 1)

                    def exp(u):
                        t.wait(s_shifted[s])
                        A(P[s][:, u % 2, :], P[s][:, u % 2, :], ACT.Exp, scale=0.25).then_inc(p_ready[s], 1)

                    def copy_pt(u):
                        t.wait(pt_psum[s])
                        if u >= 2:
                            t.wait(pv_done[s])
                        A(PT[s][:, u % 2, :], b2[0:T, 0:QW], ACT.Copy).then_inc(pt_ready[s], 1)
                    yield 4
                    exp(0)
                    yield 5
                    exp(1)
                    yield 6
                    copy_pt(0)
                    yield 7
                    exp(2)
                    yield 8
                    copy_pt(1)
                    yield 9
                    exp(3)
                    yield 10
                    copy_pt(2)
                    yield 12
                    copy_pt(3)
                    yield 15
                    t.wait(ot_psum[s])
                    for m2 in range(C2):
                        m = A(OT[s][:, m2, :], b2[:, m2 * T:(m2 + 1) * T], ACT.Identity, bias=wc(s, "bv")[:, m2:m2 + 1])
                    m.then_inc(ot_ready[s], 1)
                    yield 17
                    t.wait(xt_psum[s])
                    for m2 in range(C2):
                        m = A(ZT[s][:, m2, :], b2[:, m2 * T:(m2 + 1) * T], ACT.Identity, scale=wc(s, "n1w")[:, m2:m2 + 1], bias=wc(s, "n1b")[:, m2:m2 + 1])
                    m.then_inc(xt_ready[s], 1)
                    for g in range(FT // 2):
                        yield 18 + g
                        t.wait(h_psum[s])
                        for j in range(2):
                            mt = 2 * g + j
                            m = A(HT[s][:, mt, :], hidden_banks[s][g][:, j * T:(j + 1) * T], ACT.Relu, bias=wc(s, "b1")[:, mt:mt + 1])
                        m.then_inc(h_ready[s], 1)
                run_slots(act, B, batch, BEATS_B)

            @block.vector
            def _(dve):
                v = nc.vector
                t = Tally(dve)
                chain = route_vec

                def step(ins):
                    ins.then_inc(chain, 1)
                    t.wait(chain)

                dve.wait_ge(route_dma, 16 * 2)
                dve.wait_ge(added, 16)
                v.memset(items[:, NI:NI + 1], -1)
                v.memset(items[:, NI + 1 + B:NI + 2 + B], -1)
                for s in SLOTS:
                    v.memset(V16[s][:, :, 16:17], 1.0)
                v.memset(onesq[:, :], 1.0)
                v.tensor_copy(vals[:, :, 1], bidx[:, 1:1 + E])
                v.tensor_copy(vals[:, :, 0], bidx[:, 0:1].to_broadcast((B, E)))
                step(v.tensor_tensor(lgt[:, :], lgt[:, :], gbt[:, :], ALU.add))
                mine = lgt[:, :].unsqueeze(2).to_broadcast((B, E, E))
                other = lgt[:, :].unsqueeze(1).to_broadcast((B, E, E))
                v.tensor_tensor(cmp1[:, :, :], other, mine, ALU.is_gt)
                step(v.tensor_tensor(cmp2[:, :, :], other, mine, ALU.is_equal))
                step(v.tensor_tensor(cmp2[:, :, :], cmp2[:, :, :], lower, ALU.mult))
                step(v.tensor_tensor(cmp1[:, :, :], cmp1[:, :, :], cmp2[:, :, :], ALU.add))
                step(v.tensor_reduce(rank[:, :], cmp1[:, :, :], AX_X, ALU.add))
                v.tensor_reduce(gmax[:, :], lgt[:, :], AX_X, ALU.max, negate=True)
                v.tensor_scalar(member[:, :], rank[:, :], TOPK - 0.5, None, ALU.is_lt).then_inc(route_act, 1)
                dve.wait_ge(route_act, 1)
                v.tensor_scalar(gw[:, :], lgt[:, :], gmax[:, :], None, ALU.add).then_inc(gate_shifted, 1)
                dve.wait_ge(route_pe, 1)
                step(v.tensor_copy(tot[:, :], bank[0][1][0:B, 0:E]))
                step(v.tensor_copy(pos[:, :], bank[0][0][0:B, 0:E]))
                for e in range(1, E):
                    step(v.tensor_scalar(pos[:, e:E], pos[:, e:E], tot[:, e - 1:e], None, ALU.add))
                for e in range(E):
                    step(v.tensor_scalar(onehot[:, e, :], iota, pos[:, e:e + 1], member[:, e:e + 1], ALU.is_equal, ALU.mult))
                dve.wait_ge(gate_exp, 1)
                step(v.reciprocal(gsum[:, :], gsum[:, :]))
                v.tensor_scalar(vals[:, :, 2], gexp[:, :], gsum[:, :], None, ALU.mult).then_inc(route_act, 1)
                dve.wait_ge(route_pe, 2)
                step(v.tensor_copy(listf[:, :], bank[0][2][0:3, 0:NI]))
                v.tensor_copy(listi[:, :], listf[0:2, :]).then_inc(routed, 1)
                dve.wait_ge(routed, 2)

                def batch(s, at):
                    t = Tally(dve)
                    b0, b1, b2, b3 = bank[s]

                    def chained(ins):
                        ins.then_inc(vec_done[s], 1)
                        t.wait(vec_done[s])

                    def layernorm():
                        chained(v.bn_stats(st6[s][:, :], X[s][:, :]))
                        chained(v.bn_aggr(mv[s][:, :], st6[s][:, :]))
                        v.tensor_scalar(var[s][:, :], mv[s][:, 1:2], EPS, None, ALU.add).then_inc(ln_var[s], 1)

                    def normalise(dst):
                        t.wait(ln_rstd[s])
                        return v.tensor_scalar(dst[s][:, :], X[s][:, :], mv[s][:, 0:1], rstd[s][:, :], ALU.subtract, ALU.mult)

                    def scale_shift(src, wname, bname):
                        chained(v.tensor_tensor(Z[s][:, :], src[s][:, :], rr(s, wname), ALU.mult))
                        chained(v.tensor_tensor(Z[s][:, :], Z[s][:, :], rr(s, bname), ALU.add))

                    yield 2
                    dve.wait_ge(go[s], at.n[s] + base)
                    dve.nop().then_inc(started[s], 1)
                    dve.wait_ge(go_last[s], at.n[s] + 1)
                    dve.nop().then_inc(last_started[s], 1)
                    t.wait(m_in[s], 16)
                    v.tensor_tensor(X[s][:, :], XIN[s][:, :], rr(s, "ob"), ALU.add).then_inc(m_taken[s], 1)
                    t.wait(qkv_psum[s])
                    for u in range(4):
                        c, half_ = u // 2, slice(4 * (u % 2), 4 * (u % 2) + 4)
                        v.scalar_tensor_tensor(out=KM[s][:, c, half_, :], in0=b2[:, c * T:(c + 1) * T].unsqueeze(1).to_broadcast((128, 4, T)),
                                               scalar=wc(s, "bk")[:, c:c + 1], in1=hm8[:, half_, :],
                                               op0=ALU.add, op1=ALU.mult).then_inc(masked_ready[s], 1)
                    for u in range(4):
                        yield 4 + (0, 1, 3, 5)[u]
                        t.wait(s_psum[s])
                        sc = bank[s][u % 2][0:T, 0:QW].rearrange("p (h k) -> p h k", h=4)
                        if u >= 2:
                            t.wait(pt_psum[s])
                        top = mx[s][:, 4 * (u % 2):4 * (u % 2) + 4]
                        chained(v.tensor_reduce(top, sc, AX_X, ALU.max))
                        v.tensor_tensor(P[s][:, u % 2, :].rearrange("p (h k) -> p h k", h=4), sc,
                                        top.unsqueeze(2).to_broadcast((T, 4, T)), ALU.subtract).then_inc(s_shifted[s], 1)
                    yield 14
                    t.wait(o_psum[s])
                    o = b3[0:T, 0:H * 17].rearrange("p (h d) -> p h d", h=H)
                    chained(v.reciprocal(rec[s][:, :], o[:, :, 16]))
                    v.tensor_tensor(ON[s][:, :].rearrange("p (h d) -> p h d", h=H), o[:, :, 0:16],
                                    rec[s][:, :].unsqueeze(2).to_broadcast((T, H, 16)), ALU.mult).then_inc(on_ready[s], 1)
                    yield 16
                    t.wait(y_psum[s])
                    t.wait(m_taken[s])
                    chained(v.tensor_tensor(X[s][:, :], X[s][:, :], b0[0:T, 0:D], ALU.add))
                    layernorm()
                    yield 17
                    normalise(ZN).then_inc(xn_ready[s], 1)
                    t.wait(xn_ready[s])
                    yield 19
                    scale_shift(ZN, "n1w", "n1b")
                    chained(v.tensor_tensor(Z[s][:, :], Z[s][:, :], rr(s, "l2b"), ALU.add))
                    yield 24
                    t.wait(y_psum[s])
                    chained(v.tensor_tensor(X[s][:, :], Z[s][:, :], b3[0:T, 0:D], ALU.add))
                    layernorm()
                    yield 25
                    chained(normalise(ZN))
                    scale_shift(ZN, "n2w", "n2b")
                    dve.wait_ge(added, at.n[s] * 32 + 16)
                    v.tensor_scalar(Y[s][:, :], Z[s][:, :], gates[:, bass.ds(at.n[s] + s * B, 1)], None, ALU.mult).then_inc(y_ready[s], 1)
                run_slots(dve, B, batch, BEATS_B)

            @block.gpsimd
            def _(pool):
                g = nc.gpsimd
                g.memset(nhalf[:, :], -0.5).then_inc(halves_ready, 1)
                pool.wait_ge(halves_ready, 2)
                g.dma_start(rt[:, :], rtc).then_inc(added, 16)
                pool.wait_ge(routed, 2)

                def batch(s, at):
                    t = Tally(pool)

                    def inverse_root():
                        t.wait(ln_var[s])
                        g.tensor_tensor(rstd[s][:, :], var[s][:, :], nhalf[:, :], ALU.pow).then_inc(ln_rstd[s], 1)

                    yield 2
                    pool.wait_ge(go_last[s], at.n[s] + 1)
                    pool.nop().then_inc(last_started[s], 1)
                    yield 16
                    inverse_root()
                    yield 24
                    inverse_root()
                    yield 25
                    b = pool.value_load(items[0:1, bass.ds(at.n[s] + s * B, 1)], min_val=0, max_val=B - 1)
                    t.wait(y_ready[s])
                    g.nop().then_inc(y_taken[s], 1)
                    pool.wait_ge(added, at.n[s] * 32 + (32 if s == 0 else 16))
                    g.dma_start(out[bass.ds(b, 1), :, :].rearrange("a t d -> (a t) d"), Y[s][:, :],
                                accum_op=ALU.add).then_inc(added, 16)
                run_slots(pool, B, batch, BEATS_B)




def _chunks(a):
    import numpy as np
    n = a.shape[0] // 128
    return np.ascontiguousarray(a.reshape(n, 128, -1).transpose(1, 0, 2).reshape(128, -1))


def _cols(v):
    import numpy as np
    return np.ascontiguousarray(v.reshape(-1, 128).T)


def _pack(i):
    import numpy as np
    f = {k: np.asarray(v) for k, v in i.items()}
    cat = np.concatenate
    rep = lambda a, t: cat([a[:, t * 32:(t + 1) * 32]] * 4, 1)
    kd = f["L1_attn_wk_down"]
    wa = {"qkv0": cat([f["L0_attn_w_q"], f["L0_attn_w_k"], f["L0_attn_w_v"]], 1), "o0": f["L0_attn_w_o"],
          "xq": f["L0_xattn_Wq"], "xk": f["L0_xattn_Wk"], "xv": f["L0_xattn_Wv"], "xo": f["L0_xattn_Wo"],
          "f1": f["L0_ffn_W1"].T, "f2": f["L0_ffn_W2"].T, "k1": cat([rep(kd, 0), rep(kd, 1)], 1),
          "v1": f["L1_attn_wv_down"], "yq": f["L1_xattn_Wq"].T, "yk": f["L1_xattn_Wk"].T, "yv": f["L1_xattn_Wv"].T,
          "yo": f["L1_xattn_Wo"].T, "gate": f["L1_ffn_gate_w"].T}
    wa = cat([_chunks(wa[n]) for n, _ in WA_PARTS], 1)
    ca = {"xbq": f["L0_xattn_bq"], "xbk": f["L0_xattn_bk"], "xbv": f["L0_xattn_bv"], "fb1": f["L0_ffn_b1"],
          "qnw": f["L1_xattn_qn_w"], "qnb": f["L1_xattn_qn_b"], "cnw": f["L1_xattn_cn_w"], "cnb": f["L1_xattn_cn_b"],
          "ybq": f["L1_xattn_bq"], "ybk": f["L1_xattn_bk"], "ybv": f["L1_xattn_bv"],
          "scale": np.broadcast_to(f["L0_ffn_scale"], (128,))}
    ca = cat([_cols(ca[n]) for n, _ in CA_PARTS], 1)
    ra = cat([f["L0_xattn_bo"], f["L0_ffn_b2"], f["L1_xattn_bo"]])[None]
    wqt = f["L1_attn_wq"].reshape(D, 8, 128).transpose(2, 1, 0)
    wo = f["L1_attn_wo"].reshape(8, 128, D).transpose(1, 0, 2)
    up = [f["L1_attn_wk_up"].T, f["L1_attn_wv_up"].T]
    for p in range(4):
        up += [wqt[:, 2 * p], wqt[:, 2 * p + 1], wo[:, 2 * p], wo[:, 2 * p + 1]]
    up = cat(up, 1)
    qkvb = f["L1_ffn_in_proj_b"]
    we = [{"qkv": _chunks(f["L1_ffn_in_proj_w"][e].T), "bq": _cols(qkvb[e][0:D]), "bk": _cols(qkvb[e][D:2 * D]),
           "bv": _cols(qkvb[e][2 * D:]), "b1": _cols(f["L1_ffn_lin1_b"][e]), "n1w": _cols(f["L1_ffn_ln1_w"][e]),
           "n1b": _cols(f["L1_ffn_ln1_b"][e]), "o": _chunks(f["L1_ffn_out_proj_w"][e].T),
           "l1": _chunks(f["L1_ffn_lin1_w"][e].T), "l2": _chunks(f["L1_ffn_lin2_w"][e].T)} for e in range(E)]
    we = [cat([parts[n] for n, _ in WE_PARTS], 1) for parts in we]
    re_ = cat([f["L1_ffn_" + n] for n in ("out_proj_b", "ln1_w", "ln1_b", "lin2_b", "ln2_w", "ln2_b")], 1)
    q, d = np.arange(T, dtype=np.float32), np.arange(0, 16, 2, dtype=np.float32)
    inv = (np.float32(1.0) / np.float32(10000.0) ** (d / np.float32(16))).astype(np.float32)
    fr = (q[:, None] * inv[None, :]).astype(np.float32)
    kc = np.zeros((128, NKC), np.float32)
    kc[:, KC["ident"][0]:KC["ident"][1]] = np.eye(128)
    kc[:, KC["hm8"][0]:KC["hm8"][1]] = np.repeat(np.arange(128)[:, None] // 16 == np.arange(8)[None], T, axis=1)
    kc[0:T, KC["tri"][0]:KC["tri"][1]] = np.triu(np.ones((T, T)))
    kc[0:T, KC["cos"][0]:KC["cos"][1]] = np.tile(np.cos(fr), (1, 2))
    kc[0:T, KC["sin"][0]:KC["sin"][1]] = cat([-np.sin(fr), np.sin(fr)], 1)
    kc[:, KC["ones"][0]:KC["ones"][1]] = 1.0
    kb = np.zeros((T, T + QW + T), np.float32)
    kb[:, 0:T] = np.eye(T)
    kb[:, T:T + QW] = np.tile(np.triu(np.full((T, T), NEG), 1), (1, 4))
    kb[:, T + QW:] = 1.0
    j = np.arange(B)
    rtc = cat([np.broadcast_to(np.arange(2 * B), (B, 2 * B)), j[:, None] < j[None], np.broadcast_to(np.tril(np.ones((E, E)), -1).reshape(1, -1), (B, E * E)),
               j[:, None], np.broadcast_to(np.arange(E), (B, E))], 1).astype(np.float32)
    x, c = f["x"], f["ctx_1024"]
    return {"x": x, "ctx": c, "mask": f["mask_BxS2_bk0"].astype(np.int32), "wa": wa, "ca": ca, "ra": ra, "up": up,
            "we": np.stack(we), "re": re_, "gb": f["L1_ffn_gate_b"][None], "kc": kc, "rtc": rtc, "kb": kb}


def _program(nc, arrays):
    a = {n: nc.dram_tensor("in_" + n, v.shape, mybir.dt.from_np(v.dtype), kind="ExternalInput").ap() for n, v in arrays.items()}
    out = nc.dram_tensor("out", (B, T, D), F32, kind="ExternalOutput").ap()
    xmid = nc.dram_tensor("xmid", (B, T, D), F32).ap()
    lg = nc.dram_tensor("lg", (B, E), F32).ap()
    mrow = nc.dram_tensor("mrow", (B, LC), BF16).ap()
    sel = nc.dram_tensor("sel", (4, B * TOPK), F32).ap()
    build(nc, a["x"], a["ctx"], a["mask"], a["wa"], a["ca"], a["ra"], a["up"], a["we"], a["re"], a["gb"], a["kc"], a["kb"], a["rtc"],
          out, xmid, lg, mrow, sel)


def kernel(**inputs):
    import numpy as np
    import concourse.bacc as bacc
    from concourse.bass_utils import run_bass_kernel_spmd

    arrays = {n: np.ascontiguousarray(v) for n, v in _pack(inputs).items()}
    nc = bacc.Bacc("TRN2", target_bir_lowering=False, num_devices=1)
    _program(nc, arrays)
    r = run_bass_kernel_spmd(nc, [{"in_" + n: v for n, v in arrays.items()}], core_ids=[0])
    return r.results[0]["out"]
```
